# Optimizing a Trainium2 kernel written in Bass

```python
import numpy as np
import jax
import jax.numpy as jnp

def _softmax(x, axis=-1):
    return jax.nn.softmax(x, axis=axis)

def _gelu(x):
    return jax.nn.gelu(x, approximate=True)

def _silu(x):
    return jax.nn.silu(x)

def _sigmoid(x):
    return jax.nn.sigmoid(x)

def _layernorm(x, axis=-1, eps=1e-05):
    m = jnp.mean(x, axis=axis, keepdims=True)
    v = jnp.var(x, axis=axis, keepdims=True)
    return (x - m) / jnp.sqrt(v + eps)

def _scatter_add(tgt, idx, src, axis=0):
    return tgt.at[idx].add(src)

def _segment_sum(src, seg, n):
    return jax.ops.segment_sum(src, seg, n)
kernel_name = 'mk_gnn_ffn_d1_gnn_r32_209195'

def setup_inputs(seed: int=0):
    np.random.seed(seed)
    _w = jnp.asarray

    def _rec_inputs():
        import jax
        import jax.numpy as jnp
        _gk = jax.random.key(seed)
        x = -0.0003713 + 1 * jax.random.normal(jax.random.fold_in(_gk, 1), (3125, 256), jnp.float32)
        src = jax.random.randint(jax.random.fold_in(_gk, 2), (50000,), 0, 3125, jnp.int32)
        dst = jnp.minimum((3125 * jax.random.uniform(jax.random.fold_in(_gk, 3), (50000,)) ** 2.0).astype(jnp.int32), 99999)
        _o = jnp.argsort(dst, stable=True)
        src = src[_o]
        dst = dst[_o]
        edge_type_8 = jax.random.randint(jax.random.fold_in(_gk, 12), (50000,), 0, 8, jnp.int32)
        edge_weight = jax.random.uniform(jax.random.fold_in(_gk, 13), (50000,), jnp.float32, 0.0, 1)
        return (x, src, dst, edge_type_8, edge_weight)
    x, src, dst, edge_type_8, edge_weight = _rec_inputs()

    def _L0_gnn_setup():
        import jax, jax.numpy as jnp
        import numpy as np
        N_NODES = 50000
        N_EDGES = 25000
        IN_FEAT = 256
        OUT_FEAT = 256
        NUM_RELS = 8
        NUM_BASES = 8
        SUBMAT_IN = IN_FEAT // NUM_BASES
        SUBMAT_OUT = OUT_FEAT // NUM_BASES
        key = jax.random.key(seed)
        k_h, k_w, k_src, k_dst, k_rel, k_norm = jax.random.split(key, 6)
        h = jax.random.normal(k_h, (N_NODES, IN_FEAT), dtype=jnp.float32)
        weight = jax.random.normal(k_w, (NUM_RELS, NUM_BASES * SUBMAT_IN * SUBMAT_OUT), dtype=jnp.float32) * 0.05
        edge_src = jax.random.randint(k_src, (N_EDGES,), 0, N_NODES, dtype=jnp.int32)
        edge_dst = jax.random.randint(k_dst, (N_EDGES,), 0, N_NODES, dtype=jnp.int32)
        edge_rel = jax.random.randint(k_rel, (N_EDGES,), 0, NUM_RELS, dtype=jnp.int32)
        edge_norm = jax.random.uniform(k_norm, (N_EDGES,), dtype=jnp.float32)
        return {'h': h, 'weight': weight, 'edge_src': edge_src, 'edge_dst': edge_dst, 'edge_rel': edge_rel, 'edge_norm': edge_norm}
    _L0_gnn_all = _L0_gnn_setup()
    _L0_gnn_in = {k: v for k, v in _L0_gnn_all.items() if k in ('weight',)}
    del _L0_gnn_all

    def _L0_ffn_setup():
        import jax, jax.numpy as jnp
        import numpy as np
        E = 8
        K = 2
        D = 256
        H = 512
        DOUT = 256
        EPS = 1e-05
        key = jax.random.key(seed)
        ks = jax.random.split(key, 9)
        s = 0.02
        return {'x': jax.random.normal(ks[0], (4, 256, D), jnp.float32), 'gamma': 1.0 + 0.05 * jax.random.normal(ks[1], (D,), jnp.float32), 'beta': 0.05 * jax.random.normal(ks[2], (D,), jnp.float32), 'Wr': 0.01 * jax.random.normal(ks[3], (D, E), jnp.float32), 'br': jnp.zeros((E,), jnp.float32), 'W1': s * jax.random.normal(ks[4], (E, D, H), jnp.float32), 'b1': s * jax.random.normal(ks[5], (E, H), jnp.float32), 'W2': s * jax.random.normal(ks[6], (E, H, DOUT), jnp.float32), 'b2': s * jax.random.normal(ks[7], (E, DOUT), jnp.float32)}
    _L0_ffn_all = _L0_ffn_setup()
    _L0_ffn_in = {k: v for k, v in _L0_ffn_all.items() if k in ('gamma', 'beta', 'Wr', 'br', 'W1', 'b1', 'W2', 'b2')}
    del _L0_ffn_all
    return {'x': x, 'src': src, 'dst': dst, 'edge_type_8': edge_type_8, 'edge_weight': edge_weight, 'L0_gnn_weight': _L0_gnn_in['weight'], 'L0_ffn_gamma': _L0_ffn_in['gamma'], 'L0_ffn_beta': _L0_ffn_in['beta'], 'L0_ffn_Wr': _L0_ffn_in['Wr'], 'L0_ffn_br': _L0_ffn_in['br'], 'L0_ffn_W1': _L0_ffn_in['W1'], 'L0_ffn_b1': _L0_ffn_in['b1'], 'L0_ffn_W2': _L0_ffn_in['W2'], 'L0_ffn_b2': _L0_ffn_in['b2']}

def reference(x, src, dst, edge_type_8, edge_weight, L0_gnn_weight, L0_ffn_gamma, L0_ffn_beta, L0_ffn_Wr, L0_ffn_br, L0_ffn_W1, L0_ffn_b1, L0_ffn_W2, L0_ffn_b2):
    import jax
    import jax.numpy as jnp

    def _L0_gnn_ref(h, weight, edge_src, edge_dst, edge_rel, edge_norm):
        import jax, jax.numpy as jnp
        import numpy as np
        N_NODES = 50000
        N_EDGES = 25000
        IN_FEAT = 256
        OUT_FEAT = 256
        NUM_RELS = 8
        NUM_BASES = 8
        SUBMAT_IN = IN_FEAT // NUM_BASES
        SUBMAT_OUT = OUT_FEAT // NUM_BASES
        'RGCNBlockLayer forward (self_loop=False, bias=None, activation=None).\n\n            Per relation r: agg_r[v] = sum_{(u->v) in rel r} norm_e * h[u]\n            then block-diagonal matmul out_r = blockmm(agg_r, W_r); output = sum_r out_r.\n            '
        N, in_feat = h.shape
        R = weight.shape[0]
        msg = h[edge_src] * edge_norm[:, None]
        seg = edge_rel * N + edge_dst
        agg = jax.ops.segment_sum(msg, seg, num_segments=R * N)
        agg = agg.reshape(R, N, NUM_BASES, SUBMAT_IN)
        W = weight.reshape(R, NUM_BASES, SUBMAT_IN, SUBMAT_OUT)
        out = jnp.einsum('rnbi,rbio->nbo', agg, W)
        return out.reshape(N, NUM_BASES * SUBMAT_OUT)

    def _L0_ffn_ref(x, gamma, beta, Wr, br, W1, b1, W2, b2):
        import jax, jax.numpy as jnp
        import numpy as np
        E = 8
        K = 2
        D = 256
        H = 512
        DOUT = 256
        EPS = 1e-05
        mu = jnp.mean(x, axis=-1, keepdims=True)
        var = jnp.mean(jnp.square(x - mu), axis=-1, keepdims=True)
        xn = (x - mu) * jax.lax.rsqrt(var + EPS) * gamma + beta
        logits = jnp.einsum('bsd,de->bse', xn, Wr) + br
        top_vals, top_idx = jax.lax.top_k(logits, K)
        w = jax.nn.softmax(top_vals, axis=-1)
        w_full = jnp.einsum('bsk,bske->bse', w, jax.nn.one_hot(top_idx, E, dtype=w.dtype))
        y = jnp.zeros(x.shape[:-1] + (DOUT,), x.dtype)
        for e in range(E):
            h = jax.nn.gelu(jnp.einsum('bsd,dh->bsh', xn, W1[e]) + b1[e], approximate=False)
            y_e = jnp.einsum('bsh,hd->bsd', h, W2[e]) + b2[e]
            y = y + y_e * w_full[..., e, None]
        return y
    x = x + _L0_gnn_ref(_layernorm(x, axis=-1), L0_gnn_weight, src, dst, edge_type_8, edge_weight)
    x = x + _L0_ffn_ref(_layernorm(x, axis=-1)[None], L0_ffn_gamma, L0_ffn_beta, L0_ffn_Wr, L0_ffn_br, L0_ffn_W1, L0_ffn_b1, L0_ffn_W2, L0_ffn_b2)[0]
    return x

_drawn_inputs = setup_inputs


def setup_inputs(seed=0):
    import zlib

    import numpy as np

    out = dict(_drawn_inputs(seed))
    spreads = {'L0_ffn_br': (0.0, 0.1)}
    factors = {'L0_ffn_gamma': 7.054, 'L0_ffn_beta': 6.035, 'L0_ffn_b1': 8.0, 'L0_ffn_b2': 5.047}
    for name, (base, spread) in spreads.items():
        noise = np.random.default_rng([zlib.crc32(name.encode()), seed]).standard_normal(out[name].shape)
        drawn = base * np.exp(spread * noise) if base else spread * noise
        out[name] = jnp.asarray(drawn.astype(out[name].dtype))
    for name, factor in factors.items():
        out[name] = (out[name] * factor).astype(out[name].dtype)
    return out
```

```python
from contextlib import ExitStack

import numpy as np

import concourse.bass as bass
from concourse import mybir

F32 = mybir.dt.float32
F32R = mybir.dt.float32r
I32 = mybir.dt.int32
U32 = mybir.dt.uint32
ALU = mybir.AluOpType
ACT = mybir.ActivationFunctionType
AX = mybir.AxisListType

P = 128
N, D = 3125, 256
E = 50000
R = 8
NB = 8
SB = D // NB
X, H = 8, 512
DC, HC = D // P, H // P
EPS = 1e-5

TN = 125
NT = N // TN
GT = 3
NG = NT // GT
SLOT = P
COLS = GT * SLOT
FULL = N // P
REST = N - FULL * P
EC = (E + P - 1) // P
EB = (EC + P - 1) // P
SHORTEST = 4
ECP = EC + 2 * SHORTEST
RING = 8
LAG = 2
NEVER = 4096
FAR = 1.0e4

ORDER = [22, 23, 21, 0, 20, 19, 1, 18, 17, 2, 16, 15, 3, 14, 13, 4, 12, 11, 5, 10, 9, 6, 8, 7, 24]
PIECES = (4, 2, 2)
PARTS = {(0, "up"): (0, 0), (0, "down"): (0, 1), (1, "up"): (0, 2), (1, "down"): (0, 3),
         (2, "up"): (1, 0), (2, "down"): (1, 1), (3, "up"): (2, 0), (4, "up"): (2, 1)}
assert max(PIECES) <= SHORTEST and ECP <= EB * P
assert NT * TN == N and NG * GT + 1 == NT and sorted(ORDER) == list(range(NT))


def build_program(nc, x, src, dst, rel, norm, gnn_w, gamma, beta, wr, br, w1, b1, w2, b2,
                  starts_f, starts_i, out):
    y = nc.dram_tensor("y_rows", [N * R, D], F32).ap()
    y_nodes = y.rearrange("(n r) d -> n (r d)", r=R)

    top = ExitStack()
    with top:
        def sb(stack, name, shape, dt=F32):
            return stack.enter_context(nc.sbuf_tensor(name, shape, dt))

        def sem(name):
            return top.enter_context(nc.semaphore(name))

        bank = [top.enter_context(nc.psum_tensor(f"bank{i}", [P, 512], F32)) for i in range(8)]

        row_t = sb(top, "row_t", [P, ECP], I32)
        dst_t = sb(top, "dst_t", [P, ECP])
        norm_t = sb(top, "norm_t", [P, ECP])
        ident = sb(top, "ident", [P, P])
        iota = sb(top, "iota", [P, TN])
        starts = sb(top, "starts", [P, NT])
        starts_r = sb(top, "starts_r", [1, 32], I32)
        span_lo = sb(top, "span_lo", [1, 32], I32)
        span_n = sb(top, "span_n", [1, 32], I32)
        gam = sb(top, "gam", [P, DC])
        bet = sb(top, "bet", [P, DC])
        wr_s = sb(top, "wr_s", [P, DC, X])
        br_s = sb(top, "br_s", [P, X])
        b1_s = sb(top, "b1_s", [P, X, HC])
        b2_s = sb(top, "b2_s", [X, D])
        iota8 = sb(top, "iota8", [P, X])
        zero_r = sb(top, "zero_r", [P, TN + 1], F32R)
        stat = sb(top, "stat", [P, FULL + 1, 6])
        mv = sb(top, "mv", [P, FULL + 1, 2])
        rs = sb(top, "rs", [P, FULL + 1])
        rt = sb(top, "rt", [P, FULL + 1])
        ve = sb(top, "ve", [P, FULL + 1])

        with ExitStack() as staging:
            w_stage = sb(staging, "w_stage", [P, 2, DC * H])
        hh = sb(top, "hh", [P, 2, HC, COLS], F32R)
        hl = sb(top, "hl", [P, 2, HC, COLS], F32R)

        with ExitStack() as early:
            xall = sb(early, "xall", [P, FULL + 1, D])
            xnorm = sb(early, "xnorm", [P, 2, D])
            wbh = sb(early, "wbh", [P, DC, R, P], F32R)
            wbl = sb(early, "wbl", [P, DC, R, P], F32R)
            xph = sb(early, "xph", [P, 2, DC, P], F32R)
            xpl = sb(early, "xpl", [P, 2, DC, P], F32R)
            ybuf = sb(early, "ybuf", [P, 2, R, DC, P])
            wraw = sb(early, "wraw", [P, DC, R, P])
            e_src = sb(early, "e_src", [P, EB, P], I32)
            e_dst = sb(early, "e_dst", [P, EB, P], I32)
            e_rel = sb(early, "e_rel", [P, EB, P], I32)
            e_norm = sb(early, "e_norm", [P, EB, P])
            rowf = sb(early, "rowf", [P, EB, P])
            dstf = sb(early, "dstf", [P, EB, P])
            diag = sb(early, "diag", [P, 2, P])
            iota_t = sb(early, "iota_t", [NT, EC])
            hit = sb(early, "hit", [NT, EC])
            hit2 = sb(early, "hit2", [NT, EC])
            ones = sb(early, "ones", [P, NT])
            mnmx = sb(early, "mnmx", [P, 2, EB])
            ends = sb(early, "ends", [NT, 2])
            lohi = sb(early, "lohi", [NT, 4])
            lohi_i = sb(early, "lohi_i", [NT, 2], I32)

        w1h = sb(top, "w1h", [P, DC, X, H], F32R)
        w1l = sb(top, "w1l", [P, DC, X, H], F32R)
        w2h = sb(top, "w2h", [P, HC, X, D], F32R)
        w2l = sb(top, "w2l", [P, HC, X, D], F32R)
        gath = sb(top, "gath", [P, 2 * RING, D])
        idx = sb(top, "idx", [P, 2 * RING], I32)
        m_ab = sb(top, "m_ab", [P, 2, TN])
        iota_s = sb(top, "iota_s", [P, TN])
        act_h = sb(top, "act_h", [P, 2, COLS])
        xtf = sb(top, "xtf", [P, DC, COLS])
        xth = sb(top, "xth", [P, 2, DC, COLS], F32R)
        xtl = sb(top, "xtl", [P, 2, DC, COLS], F32R)
        xz = sb(top, "xz", [P, GT, D])
        x1 = sb(top, "x1", [P, 2, GT, D])
        logit = sb(top, "logit", [P, GT, X])
        mx8 = sb(top, "mx8", [P, GT, X])
        ix8 = sb(top, "ix8", [P, GT, X], U32)
        ixf = sb(top, "ixf", [P, GT, X])
        dlt = sb(top, "dlt", [P, GT])
        tnh = sb(top, "tnh", [P, GT])
        w12 = sb(top, "w12", [P, 2, GT])
        wfull = sb(top, "wfull", [P, GT, X])
        wft = xtf[0:X, :, :].rearrange("p c n -> p (c n)")

        ld_edge = sem("ld_edge")
        ld_x = sem("ld_x")
        ld_wb = sem("ld_wb")
        ld_small = sem("ld_small")
        ld_w1 = sem("ld_w1")
        ld_w2 = sem("ld_w2")
        pool_const = sem("pool_const")
        fill = sem("fill")
        edge_f = sem("edge_f")
        diag_rdy = sem("diag_rdy")
        pe_edge = sem("pe_edge")
        span_col = sem("span_col")
        span_rdy = sem("span_rdy")
        dve_seq = sem("dve_seq")
        dve_go = sem("dve_go")
        xhat_rdy = sem("xhat_rdy")
        wb_h = sem("wb_h")
        wb_l = sem("wb_l")
        xp_t = sem("xp_t")
        xp_h = sem("xp_h")
        xp_l = sem("xp_l")
        y_mm = sem("y_mm")
        y_ev_a = sem("y_ev_a")
        y_ev_v = sem("y_ev_v")
        y_st = [sem(f"y_st{i}") for i in range(2)]
        w_h = sem("w_h")
        w_l = sem("w_l")
        early_done = sem("early_done")
        idx_rdy = sem("idx_rdy")
        land = [sem(f"land{i}") for i in range(RING)]
        landed = sem("landed")
        pair_used = sem("pair_used")
        a_used = sem("a_used")
        m_rdy = sem("m_rdy")
        iota_rdy = sem("iota_rdy")
        ld_xin = [sem(f"ld_xin{i}") for i in range(GT)]
        acc_rdy = sem("acc_rdy")
        x1_rdy = sem("x1_rdy")
        z_rdy = sem("z_rdy")
        t_made = sem("t_made")
        t_read = sem("t_read")
        xt_rdy = sem("xt_rdy")
        wf_rdy = sem("wf_rdy")
        wft_rdy = sem("wft_rdy")
        dlt_rdy = sem("dlt_rdy")
        tnh_rdy = sem("tnh_rdy")
        b_mm = sem("b_mm")
        b_add = sem("b_add")
        h_mm = sem("h_mm")
        h_act = sem("h_act")
        h_split = sem("h_split")
        y2_mm = sem("y2_mm")
        y2_add = sem("y2_add")
        st_out = [sem(f"st_out{i}") for i in range(GT)]

        bank_y, bank_tp = bank[0:4], bank[4:6]
        bank_h, bank_o, bank_acc, bank_t = bank[0:2], bank[2:5], bank[5:7], bank[7]

        gnn_v = gnn_w.rearrange("r (b i o) -> b i r o", b=NB, i=SB)
        w1_v = w1.rearrange("e (c p) h -> e p c h", p=P)
        w2_v = w2.rearrange("e (c p) d -> e p c d", p=P)
        n_small = 9
        full_rows = E // P
        rest_e = E - full_rows * P
        eb_full = full_rows // P
        eb_rest = full_rows - eb_full * P

        def part_of(engine, g, k, part, parts):
            n = engine.value_load(span_n[0:1, bass.ds(g * GT + k, 1)], min_val=SHORTEST, max_val=NEVER)
            return n if parts == 1 else (n + part) // parts

        block = top.enter_context(nc.Block())

        @block.sync
        def _(sp):
            sp.sem_inc(y_st[1], 16)
            for k in range(GT):
                sp.sem_inc(st_out[k], 16)
            sp.wait_ge(fill, 2)
            for a, t in ((src, e_src), (dst, e_dst), (rel, e_rel), (norm, e_norm)):
                rows = a[0:full_rows * P].rearrange("(t p) -> t p", p=P)
                sp.dma_start(t[:, 0:eb_full, :],
                             rows[0:eb_full * P].rearrange("(b t) p -> t b p", t=P)).then_inc(ld_edge, 16)
                sp.dma_start(t[0:eb_rest, eb_full, :], rows[eb_full * P:full_rows]).then_inc(ld_edge, 16)
                sp.dma_start(t[eb_rest:eb_rest + 1, eb_full, 0:rest_e],
                             a[full_rows * P:E].rearrange("(a n) -> a n", a=1)).then_inc(ld_edge, 16)
            q = FULL // 4
            for c in range(4):
                sp.dma_start(xall[:, c * q:(c + 1) * q, :],
                             x[c * q * P:(c + 1) * q * P, :].rearrange("(t p) d -> p t d", p=P)).then_inc(ld_x, 16)
            sp.dma_start(xall[0:REST, FULL, :], x[FULL * P:N, :]).then_inc(ld_x, 16)
            for e in range(2):
                (sp.dma_start(w_stage[:, 0, :].rearrange("p (c h) -> p c h", c=DC), w1_v[0]).then_inc(ld_w1, 16)
                 if e == 0 else
                 sp.dma_start(w_stage[:, 1, :].rearrange("p (c d) -> p c d", c=HC), w2_v[0]).then_inc(ld_w2, 16))

            def store_y(t, i, par):
                sp.wait_ge(y_ev_a, t * 2 + 2)
                sp.wait_ge(y_ev_v, t * 2 + 2)
                sp.dma_start(y_nodes[bass.ds(t * P, P), :],
                             ybuf[:, par, :, :, :].rearrange("p r c g -> p (r c g)")).then_inc(y_st[par], 16)

            with sp.Fori(0, FULL // 2) as i:
                store_y(i * 2, i, 0)
                store_y(i * 2 + 1, i, 1)
            sp.wait_ge(y_ev_a, FULL * 2 + 2)
            sp.wait_ge(y_ev_v, FULL * 2 + 2)
            yb = ybuf[:, FULL % 2, :, :, :].rearrange("p r c g -> p (r c g)")
            k = REST // 16 * 16
            sp.dma_start(y_nodes[FULL * P:FULL * P + k, :], yb[0:k, :]).then_inc(y_st[FULL % 2], 16)
            sp.dma_start(y_nodes[FULL * P + k:N, :], yb[k:REST, :]).then_inc(y_st[FULL % 2], 16)

            def load_xin(g, k):
                start = sp.value_load(starts_r[0:1, bass.ds(g * GT + k, 1)], min_val=0, max_val=N - TN)
                sp.dma_start(xz[0:TN, k, :], x[bass.ds(start, TN), :]).then_inc(ld_xin[k], 16)

            sp.wait_ge(y_st[0], 16 * (FULL // 2) + 32)
            sp.wait_ge(y_st[1], 16 + 16 * (FULL // 2))
            sp.wait_ge(ld_small, 16 * n_small)
            for k in range(GT):
                load_xin(0, k)
            with sp.Fori(1, X) as e:
                sp.wait_ge(w_l, e * 2 - 1)
                sp.dma_start(w_stage[:, 0, :].rearrange("p (c h) -> p c h", c=DC),
                             w1_v[bass.ds(e, 1)].rearrange("a p c h -> p (a c) h")).then_inc(ld_w1, 16)
                sp.wait_ge(w_l, e * 2)
                sp.dma_start(w_stage[:, 1, :].rearrange("p (c d) -> p c d", c=HC),
                             w2_v[bass.ds(e, 1)].rearrange("a p c d -> p (a c) d")).then_inc(ld_w2, 16)

            def store_out(g, par, tiles):
                for k in range(tiles):
                    sp.wait_ge(y2_add, GT + g * (GT * X) + (X - 1) * tiles + k + 1)
                    start = sp.value_load(starts_r[0:1, bass.ds(g * GT + k, 1)], min_val=0, max_val=N - TN)
                    sp.dma_start(out[bass.ds(start, TN), :], x1[0:TN, par, k, :]).then_inc(st_out[k], 16)

            def load_group(g, tiles):
                sp.wait_ge(t_made, g * 4 - 2)
                for k in range(tiles):
                    load_xin(g, k)

            load_group(1, GT)
            with sp.Fori(0, (NG - 2) // 2) as i:
                for par in range(2):
                    load_group(i * 2 + par + 2, GT)
                    store_out(i * 2 + par, par, GT)
            load_group(NG, 1)
            for g in range(NG - 2, NG):
                store_out(g, g % 2, GT)
            store_out(NG, NG % 2, 1)
            sp.wait_ge(st_out[0], 16 * (NG + 2))
            for k in range(1, GT):
                sp.wait_ge(st_out[k], 16 * (NG + 1))

        @block.gpsimd
        def _(pool):
            pool.memset(ident[:, :], 0.0).then_inc(pool_const, 1)
            pool.wait_ge(pool_const, 1)
            pool.affine_select(out=ident[:, :], in_=ident[:, :], compare_op=ALU.not_equal, fill=1.0,
                               base=0, pattern=[[-1, P]], channel_multiplier=1).then_inc(pool_const, 1)
            pool.iota(iota[:, :], pattern=[[1, TN]], base=0, channel_multiplier=0,
                      allow_small_or_imprecise_dtypes=True).then_inc(pool_const, 1)
            pool.iota(iota8[:, :], pattern=[[1, X]], base=0, channel_multiplier=0,
                      allow_small_or_imprecise_dtypes=True).then_inc(pool_const, 1)
            pool.iota(iota_t[:, :], pattern=[[1, EC]], base=0, channel_multiplier=0,
                      allow_small_or_imprecise_dtypes=True).then_inc(pool_const, 1)
            pool.sem_inc(pair_used, RING)
            pool.wait_ge(span_rdy, 1)
            total = pool.alloc_register("total")
            pool.reg_mov(total, RING - 1)
            with pool.Fori(0, NT) as i:
                n = pool.value_load(span_n[0:1, bass.ds(i, 1)], min_val=SHORTEST, max_val=NEVER)
                pool.reg_add(total, total, n)
            pool.reg_alu(total, total, RING.bit_length() - 1, ALU.logical_shift_right)
            turns = pool.snap(total, min_val=NT * SHORTEST // RING, max_val=NEVER * NT)
            col = pool.alloc_register("col")
            left = pool.alloc_register("left")
            at = pool.alloc_register("at")
            pool.reg_mov(at, 0)
            pool.reg_load(col, span_lo[0:1, 0:1])
            pool.reg_load(left, span_n[0:1, 0:1])
            pool.wait_ge(y_st[0], 16 * (FULL // 2) + 32)
            pool.wait_ge(y_st[1], 16 + 16 * (FULL // 2))

            def gather_pair(turn, j, first=False):
                pool.wait_ge(pair_used, turn * RING + j + 1)
                c = pool.snap(col, min_val=0, max_val=EC - 1)
                pool.tensor_copy(idx[:, 2 * j:2 * j + 2], row_t[:, bass.ds(c, 2)]).then_inc(idx_rdy, 1)
                pool.reg_add(col, col, 2)
                pool.reg_sub(left, left, 1)
                with pool.If_eq(left, 0):
                    pool.reg_add(at, at, 1)
                    a = pool.snap(at, min_val=0, max_val=NT)
                    pool.reg_load(col, span_lo[0:1, bass.ds(a, 1)])
                    pool.reg_load(left, span_n[0:1, bass.ds(a, 1)])
                pool.wait_ge(idx_rdy, turn * RING + j + 1)
                if not first:
                    pool.wait_ge(land[(j - LAG) % RING], turn * 32 + (32 if j >= LAG else 0))
                pool.sem_inc(landed, 1)
                for s in (2 * j, 2 * j + 1):
                    pool.indirect_dma_start(
                        out=gath[:, s, :], out_offset=None, in_=y,
                        in_offset=bass.IndirectOffsetOnAxis(ap=idx[:, s:s + 1], axis=0),
                    ).then_inc(land[j], 16)
            for j in range(RING):
                gather_pair(0, j, j < LAG)
            with pool.Fori(1, turns) as turn:
                for j in range(RING):
                    gather_pair(turn, j)
            for j in range(LAG):
                pool.wait_ge(land[RING - LAG + j], turns * 32)
                pool.sem_inc(landed, 1)
            for j in range(RING):
                pool.wait_ge(land[j], turns * 32)

        @block.tensor
        def _(pe):
            def split_mm(outp, stat_h, stat_l, mov_h, mov_l, start, stop):
                pe.matmul(outp, stat_h, mov_h, start=start, stop=False)
                pe.matmul(outp, stat_h, mov_l, start=False, stop=False)
                return pe.matmul(outp, stat_l, mov_h, start=False, stop=stop)

            pe.sem_inc(y2_mm, GT)
            pe.sem_inc(a_used, 1)
            pe.wait_ge(pool_const, 2)
            pe.wait_ge(edge_f, 3)
            for b, t in enumerate((rowf, dstf, e_norm)):
                for k in range(EB):
                    last = pe.transpose(bank[b][:, k * P:(k + 1) * P], t[:, k, :], ident[:, :])
                last.then_inc(pe_edge, 1)
            for i in range(2 * EB):
                pe.wait_ge(diag_rdy, i + 1)
                pe.matmul(bank[3 + i // EB][0:NT, (i % EB) * P:(i % EB + 1) * P], ones[:, :],
                          diag[:, i % 2, :], start=True, stop=True).then_inc(pe_edge, 1)
            pe.wait_ge(span_col, 1)
            for i in range(2):
                last = pe.transpose(bank[6][0:1, i * 32:i * 32 + NT], lohi[:, 2 + i:3 + i], ident[0:NT, 0:NT])
            last.then_inc(pe_edge, 1)

            def make_y(t, par, first_two=False):
                pe.wait_ge(xhat_rdy, t + 1)
                if not first_two:
                    pe.wait_ge(xp_l, t - 1)
                for c in range(DC):
                    last = pe.transpose(bank_tp[par][:, c * P:(c + 1) * P],
                                        xnorm[:, par, c * P:(c + 1) * P], ident[:, :])
                last.then_inc(xp_t, 1)

            def mul_y(t, par):
                pe.wait_ge(xp_l, t + 1)
                for u in range(4):
                    c, half = u // 2, u % 2
                    pe.wait_ge(y_ev_a if half == 0 else y_ev_v, t * 2 + c - 1)
                    split_mm(bank_y[u][:, :], xph[:, par, c, :], xpl[:, par, c, :],
                             wbh[:, c, 4 * half:4 * half + 4, :].rearrange("p r g -> p (r g)"),
                             wbl[:, c, 4 * half:4 * half + 4, :].rearrange("p r g -> p (r g)"),
                             True, True).then_inc(y_mm, 1)

            pe.wait_ge(wb_l, 1)
            pe.wait_ge(span_rdy, 1)
            make_y(0, 0, True)
            make_y(1, 1, True)
            pe.wait_ge(xp_l, 1)
            for u in range(4):
                c, half = u // 2, u % 2
                split_mm(bank_y[u][:, :], xph[:, 0, c, :], xpl[:, 0, c, :],
                         wbh[:, c, 4 * half:4 * half + 4, :].rearrange("p r g -> p (r g)"),
                         wbl[:, c, 4 * half:4 * half + 4, :].rearrange("p r g -> p (r g)"),
                         True, True).then_inc(y_mm, 1)
            with pe.Fori(0, FULL // 2 - 1) as i:
                make_y(i * 2 + 2, 0)
                mul_y(i * 2 + 1, 1)
                make_y(i * 2 + 3, 1)
                mul_y(i * 2 + 2, 0)
            make_y(FULL, 0)
            mul_y(FULL - 1, 1)
            mul_y(FULL, 0)

            pair = pe.alloc_register("pe_pair")
            slot = pe.alloc_register("pe_slot")
            pe.reg_mov(pair, 0)

            def sum_part(g, k, part, parts):
                acc = bank_acc[k % 2]
                if part == 0:
                    if not (isinstance(g, int) and g == 0 and k < 2):
                        pe.wait_ge(x1_rdy, g * GT + k - (1 if k else 0))
                    pe.matmul(acc[0:TN, 0:2], zero_r[:, 0:TN], zero_r[:, 0:2], start=True, stop=False,
                              skip_group_check=True)
                n = part_of(pe, g, k, part, parts)
                with pe.Fori(0, n):
                    p = pe.snap(pair, min_val=0, max_val=NEVER * NT)
                    pe.reg_alu(slot, pair, RING - 1, ALU.bitwise_and)
                    s = pe.snap(slot, min_val=0, max_val=RING - 1)
                    pe.wait_ge(landed, p + 1 + LAG)
                    for ab in range(2):
                        pe.wait_ge(m_rdy, p * 2 + 3 + ab)
                        pe.matmul(acc[0:TN, 0:D], m_ab[:, ab, :],
                                  gath[:, bass.ds(s * 2 + ab, 1), :].rearrange("p a d -> p (a d)"),
                                  start=False, stop=False, skip_group_check=True)\
                          .then_inc(a_used if ab == 0 else pair_used, 1)
                    pe.reg_add(pair, pair, 1)
                if part == parts - 1:
                    pe.wait_ge(ld_xin[k], g * 16 + 16)
                    pe.matmul(acc[0:TN, 0:D], ident[0:TN, 0:TN], xz[0:TN, k, :], start=False, stop=True,
                              skip_group_check=True).then_inc(acc_rdy, 1)

            def t_free(g, i):
                if not (isinstance(g, int) and g * 4 + i == 0):
                    pe.wait_ge(t_read, g * 4 + i)

            def turn_over(g, first, tiles):
                pe.wait_ge(z_rdy, g + 1)
                t_free(g, first // 2)
                for k in range(first, min(first + 2, tiles)):
                    for c in range(DC):
                        at = (k - first) * D + c * P
                        last = pe.transpose(bank_t[:, at:at + TN], xz[0:TN, k, c * P:(c + 1) * P], ident[0:TN, 0:TN])
                last.then_inc(t_made, 1)

            def route(g, tiles):
                use = (tiles + 1) // 2
                t_free(g, use)
                pe.wait_ge(xt_rdy, g * GT + tiles)
                for k in range(tiles):
                    for c in range(DC):
                        last = pe.matmul(bank_t[0:TN, k * X:(k + 1) * X], xtf[:, c, k * SLOT:k * SLOT + TN],
                                         wr_s[:, c, :], start=(c == 0), stop=(c == DC - 1))
                last.then_inc(t_made, 1)

            def turn_weights(g, tiles):
                t_free(g, (tiles + 1) // 2 + 1)
                pe.wait_ge(wf_rdy, g + 1)
                for k in range(tiles):
                    last = pe.transpose(bank_t[0:X, k * SLOT:k * SLOT + TN], wfull[0:TN, k, :], ident[0:TN, 0:TN])
                last.then_inc(t_made, 1)

            def bias2(g, tiles):
                pe.wait_ge(wft_rdy, g + 1)
                for k in range(tiles):
                    pe.wait_ge(y2_add, g * (GT * X) + (GT + k + 1))
                    pe.matmul(bank_o[k][0:TN, 0:D], wft[:, k * SLOT:k * SLOT + TN], b2_s[:, :],
                              start=True, stop=True).then_inc(b_mm, 1)

            def up(g, par, e, tiles):
                cols = tiles * SLOT
                if e == 0:
                    pe.wait_ge(xt_rdy, g * GT + tiles)
                for hc in range(HC):
                    if not (isinstance(g, int) and g * X * HC + e * HC + hc < 2):
                        pe.wait_ge(h_act, g * (X * HC) + e * HC + hc - 1)
                    for c in range(DC):
                        f = slice(hc * P, (hc + 1) * P)
                        last = split_mm(bank_h[hc % 2][:, 0:cols], w1h[:, c, e, f], w1l[:, c, e, f],
                                        xth[:, par, c, 0:cols], xtl[:, par, c, 0:cols], c == 0, c == DC - 1)
                    last.then_inc(h_mm, 1)

            def down(g, e, tiles):
                pe.wait_ge(h_split, g * (X * HC) + e * HC + HC)
                for k in range(tiles):
                    if e == 1:
                        pe.wait_ge(b_add, g * GT + k + 1)
                    if not (isinstance(g, int) and g == 0 and e == 0):
                        if tiles == GT or e:
                            pe.wait_ge(y2_add, g * (GT * X) + (GT + (e - 1) * tiles + k + 1))
                        else:
                            pe.wait_ge(y2_add, g * (GT * X) + GT)
                    for hc in range(HC):
                        f = slice(k * SLOT, k * SLOT + TN)
                        last = split_mm(bank_o[k][0:TN, 0:D], hh[:, e % 2, hc, f], hl[:, e % 2, hc, f],
                                        w2h[:, hc, e, :], w2l[:, hc, e, :], hc == 0, hc == HC - 1)
                    last.then_inc(y2_mm, 1)

            def experts(g, par, tiles, ahead):
                for e in range(X):
                    for place in ("up", "down"):
                        k, part = PARTS.get((e, place), (GT, 0))
                        if k < ahead:
                            sum_part(g + 1, k, part, PIECES[k])
                        if place == "up":
                            if e == 1:
                                bias2(g, tiles)
                            if e == X - 2 and ahead:
                                turn_over(g + 1, 0, ahead)
                            if e == X - 1 and ahead:
                                route(g + 1, ahead)
                            if e + 1 < X:
                                up(g, par, e + 1, tiles)
                            elif ahead:
                                up(g + 1, 1 - par, 0, ahead)
                        else:
                            if e == 0:
                                turn_weights(g, tiles)
                            if e == X - 2 and ahead > 2:
                                turn_over(g + 1, 2, ahead)
                            down(g, e, tiles)

            pe.wait_ge(early_done, 1)
            for k in range(GT):
                sum_part(0, k, 0, 1)
            turn_over(0, 0, GT)
            turn_over(0, 2, GT)
            route(0, GT)
            pe.wait_ge(w_l, 2 * X)
            up(0, 0, 0, GT)
            with pe.Fori(0, (NG - 2) // 2) as i:
                for par in range(2):
                    experts(i * 2 + par, par, GT, GT)
            experts(NG - 2, 0, GT, GT)
            experts(NG - 1, 1, GT, 1)
            experts(NG, 0, 1, 0)

        @block.scalar
        def _(act):
            act.dma_start(starts_r[:, 0:NT], starts_i).then_inc(ld_small, 16)
            act.dma_start(starts[:, :], starts_f.partition_broadcast(P)).then_inc(ld_small, 16)
            act.wait_ge(fill, 1)
            for b in range(NB):
                c, q = b * SB // P, b * SB % P
                act.dma_start(wraw[q:q + SB, c, :, q:q + SB], gnn_v[b]).then_inc(ld_wb, 16)
            act.dma_start(ends[:, 0:1], starts_f.rearrange("(n a) -> n a", a=1)).then_inc(ld_small, 16)
            with nc.allow_non_contiguous_dma(reason="small parameters, once"):
                act.dma_start(gam[:, :], gamma.rearrange("(c p) -> p c", p=P)).then_inc(ld_small, 16)
                act.dma_start(bet[:, :], beta.rearrange("(c p) -> p c", p=P)).then_inc(ld_small, 16)
                act.dma_start(b1_s[:, :, :].rearrange("p e c -> p (e c)"),
                              b1.rearrange("e (c p) -> p (e c)", p=P)).then_inc(ld_small, 16)
            act.dma_start(wr_s[:, :, :], wr.rearrange("(c p) e -> p c e", p=P)).then_inc(ld_small, 16)
            act.dma_start(br_s[:, :], br.partition_broadcast(P)).then_inc(ld_small, 16)
            act.dma_start(b2_s[:, :], b2).then_inc(ld_small, 16)
            act.wait_ge(ld_wb, 16 * NB)
            act.activation(wbh[:, :, :, :], wraw[:, :, :, :], ACT.Copy).then_inc(wb_h, 1)

            def part_of_y(t, par):
                act.wait_ge(xp_t, t + 1)
                act.activation(xph[:, par, :, :].rearrange("p c n -> p (c n)"), bank_tp[par][:, 0:D],
                               ACT.Copy).then_inc(xp_h, 1)

            def copy_y(t, par, u):
                act.wait_ge(y_mm, t * 4 + u + 1)
                act.activation(ybuf[:, par, 0:4, u // 2, :], bank_y[u][:, :].rearrange("p (r g) -> p r g", g=P),
                               ACT.Copy).then_inc(y_ev_a, 1)

            part_of_y(0, 0)
            part_of_y(1, 1)
            copy_y(0, 0, 0)
            copy_y(0, 0, 2)
            with act.Fori(0, FULL // 2 - 1) as i:
                for par, t in ((0, i * 2 + 2), (1, i * 2 + 3)):
                    act.wait_ge(y_mm, t * 4 - 4)
                    part_of_y(t, par)
                    if par == 1:
                        act.wait_ge(y_st[0], i * 16 + 16)
                        copy_y(t - 1, 0, 0)
                        copy_y(t - 1, 0, 2)
                    else:
                        act.wait_ge(y_st[1], 16 + i * 16)
                        copy_y(t - 1, 1, 0)
                        copy_y(t - 1, 1, 2)
            act.wait_ge(y_mm, FULL * 4 - 4)
            part_of_y(FULL, 0)
            act.wait_ge(y_st[1], 16 + (FULL // 2 - 1) * 16)
            copy_y(FULL - 1, 1, 0)
            copy_y(FULL - 1, 1, 2)
            act.wait_ge(y_st[0], (FULL // 2) * 16)
            copy_y(FULL, 0, 0)
            copy_y(FULL, 0, 2)

            for e in range(X):
                act.wait_ge(ld_w1, 16 * (e + 1))
                act.activation(w1h[:, :, e, :], w_stage[:, 0, :].rearrange("p (c h) -> p c h", c=DC),
                               ACT.Copy).then_inc(w_h, 1)
                act.wait_ge(ld_w2, 16 * (e + 1))
                act.activation(w2h[:, :, e, :], w_stage[:, 1, :].rearrange("p (c d) -> p c d", c=HC),
                               ACT.Copy).then_inc(w_h, 1)

            def take_x1(g, par, k):
                act.wait_ge(acc_rdy, g * GT + k + 1)
                if not (isinstance(g, int) and g < 2):
                    act.wait_ge(st_out[k], g * 16)
                act.activation(x1[0:TN, par, k, :], bank_acc[k % 2][0:TN, 0:D], ACT.Copy).then_inc(x1_rdy, 1)

            def gelu(g, e, tiles):
                cols = tiles * SLOT
                if not (isinstance(g, int) and g == 0 and e < 2):
                    act.wait_ge(y2_mm, g * (GT * X) + ((e - 1) * tiles + GT if e else 0))
                for hc in range(HC):
                    act.wait_ge(h_mm, g * (X * HC) + e * HC + hc + 1)
                    if not (isinstance(g, int) and g * X * HC + e * HC + hc < 2):
                        act.wait_ge(h_split, g * (X * HC) + e * HC + hc - 1)
                    act.activation(act_h[:, hc % 2, 0:cols], bank_h[hc % 2][:, 0:cols], ACT.Gelu,
                                   bias=b1_s[:, e, hc:hc + 1])
                    act.activation(hh[:, e % 2, hc, 0:cols], bank_h[hc % 2][:, 0:cols], ACT.Gelu,
                                   bias=b1_s[:, e, hc:hc + 1]).then_inc(h_act, 1)

            def tanh_of_gap(g, tiles):
                act.wait_ge(dlt_rdy, g + 1)
                act.activation(tnh[0:TN, 0:tiles], dlt[0:TN, 0:tiles], ACT.Tanh, scale=0.5).then_inc(tnh_rdy, 1)

            def experts(g, par, tiles, ahead):
                for e in range(X):
                    if e + 1 < X:
                        gelu(g, e + 1, tiles)
                    elif ahead:
                        tanh_of_gap(g + 1, ahead)
                        gelu(g + 1, 0, ahead)
                    for place in ("up", "down"):
                        k, part = PARTS.get((e, place), (GT, 0))
                        if k < ahead and part == PIECES[k] - 1:
                            take_x1(g + 1, 1 - par, k)

            act.wait_ge(ld_small, 16 * n_small)
            act.wait_ge(early_done, 1)
            for k in range(GT):
                take_x1(0, 0, k)
            tanh_of_gap(0, GT)
            gelu(0, 0, GT)
            with act.Fori(0, (NG - 2) // 2) as i:
                for par in range(2):
                    experts(i * 2 + par, par, GT, GT)
            experts(NG - 2, 0, GT, GT)
            experts(NG - 1, 1, GT, 1)
            experts(NG, 0, 1, 0)

        @block.vector
        def _(dve):
            seq = dve.alloc_register("dve_steps")
            dve.reg_mov(seq, 0)

            def chain(*steps):
                for step in steps:
                    step().then_inc(dve_seq, 1)
                    dve.reg_add(seq, seq, 1)
                    dve.wait_ge(dve_seq, dve.snap(seq, min_val=0, max_val=1 << 20))
                    dve.sem_inc(dve_go, 1)

            def rsqrt_steps(rows, n):
                v, r, t = ve[0:rows, 0:n], rs[0:rows, 0:n], rt[0:rows, 0:n]
                steps = [
                    lambda: dve.tensor_scalar(r.bitcast(I32), v.bitcast(I32), 1, None, ALU.logical_shift_right),
                    lambda: dve.tensor_scalar(r.bitcast(I32), r.bitcast(I32), -1.0, float(0x5F3759DF), ALU.mult, ALU.add),
                ]
                for _ in range(3):
                    steps += [
                        lambda: dve.tensor_tensor(t, r, r, ALU.mult),
                        lambda: dve.scalar_tensor_tensor(out=t, in0=t, scalar=-0.5, in1=v, op0=ALU.mult, op1=ALU.mult),
                        lambda: dve.scalar_tensor_tensor(out=r, in0=t, scalar=1.5, in1=r, op0=ALU.add, op1=ALU.mult),
                    ]
                return steps

            def each(tiles, f):
                def step():
                    for k in range(tiles):
                        last = f(k)
                    return last
                return step

            def statistics(rows, tiles, source, a=1.0, b=EPS):
                chain(
                    each(tiles, lambda k: dve.bn_stats(stat[0:rows, k, :], source(k))),
                    each(tiles, lambda k: dve.bn_aggr(mv[0:rows, k, :], stat[0:rows, k, :])),
                    lambda: dve.tensor_scalar(ve[0:rows, 0:tiles], mv[0:rows, 0:tiles, 1], a, b, ALU.mult,
                                              ALU.add),
                    *rsqrt_steps(rows, tiles),
                )

            def centre(rows, k, source, target):
                return dve.tensor_scalar(target, source, mv[0:rows, k, 0:1], rs[0:rows, k:k + 1],
                                         ALU.subtract, ALU.mult)

            dve.sem_inc(y2_add, GT)
            dve.sem_inc(m_rdy, 2)
            dve.memset(wraw[:, :, :, :], 0.0).then_inc(fill, 1)
            dve.memset(e_src[:, EB - 1, :], 0)
            dve.memset(e_rel[:, EB - 1, :], 0)
            dve.memset(e_dst[:, EB - 1, :], N - 1)
            dve.memset(xall[:, FULL, :], 0.0)
            dve.memset(e_norm[:, EB - 1, :], 0.0).then_inc(fill, 1)
            dve.memset(ones[:, :], 1.0)
            dve.memset(zero_r[:, :].bitcast(F32), 0.0)
            dve.memset(span_lo[:, :], 0)
            dve.memset(span_n[:, :], NEVER)

            dve.wait_ge(ld_edge, 16 * 12)
            dve.tensor_copy(rowf[:, :, :], e_src[:, :, :])
            dve.tensor_copy(dstf[:, :, :], e_dst[:, :, :]).then_inc(edge_f, 1)
            dve.wait_ge(edge_f, 1)
            dve.tensor_reduce(mnmx[:, 0, :], dstf[:, :, :], AX.X, ALU.min)
            dve.tensor_reduce(mnmx[:, 1, :], dstf[:, :, :], AX.X, ALU.max).then_inc(edge_f, 1)
            dve.scalar_tensor_tensor(out=rowf[:, :, :], in0=rowf[:, :, :], scalar=float(R), in1=e_rel[:, :, :],
                                     op0=ALU.mult, op1=ALU.add).then_inc(edge_f, 1)
            dve.wait_ge(edge_f, 3)
            dve.wait_ge(pool_const, 5)
            for i in range(2 * EB):
                if i >= 2:
                    dve.wait_ge(pe_edge, 3 + i - 1)
                dve.tensor_scalar(diag[:, i % 2, :], ident[:, :], mnmx[:, i // EB, i % EB:i % EB + 1], None,
                                  ALU.mult).then_inc(diag_rdy, 1)
            dve.wait_ge(pe_edge, 3)
            dve.tensor_copy(row_t[:, 0:ECP], bank[0][:, 0:ECP])
            dve.tensor_copy(dst_t[:, 0:ECP], bank[1][:, 0:ECP])
            dve.tensor_copy(norm_t[:, 0:ECP], bank[2][:, 0:ECP])
            dve.wait_ge(pe_edge, 3 + 2 * EB)
            dve.wait_ge(ld_small, 16 * n_small)
            chain(
                lambda: dve.tensor_scalar(ends[:, 1:2], ends[:, 0:1], float(TN), None, ALU.add),
                lambda: dve.tensor_scalar(hit[:, :], bank[4][0:NT, 0:EC], ends[:, 0:1], None, ALU.is_ge),
                lambda: dve.scalar_tensor_tensor(out=hit[:, :], in0=bank[3][0:NT, 0:EC], scalar=ends[:, 1:2],
                                                 in1=hit[:, :], op0=ALU.is_lt, op1=ALU.mult),
                lambda: dve.scalar_tensor_tensor(out=hit2[:, :], in0=iota_t[:, :], scalar=1.0, in1=hit[:, :],
                                                 op0=ALU.add, op1=ALU.mult),
                lambda: dve.tensor_reduce(lohi[:, 1:2], hit2[:, :], AX.X, ALU.max),
                lambda: dve.scalar_tensor_tensor(out=hit2[:, :], in0=hit[:, :], scalar=-FAR, in1=iota_t[:, :],
                                                 op0=ALU.mult, op1=ALU.add),
                lambda: dve.tensor_reduce(lohi[:, 0:1], hit2[:, :], AX.X, ALU.min),
                lambda: dve.tensor_scalar(lohi[:, 2:3], lohi[:, 0:1], FAR, float(EC - 1), ALU.add, ALU.min),
                lambda: dve.scalar_tensor_tensor(out=lohi[:, 3:4], in0=lohi[:, 1:2], scalar=1.0, in1=lohi[:, 2:3],
                                                 op0=ALU.add, op1=ALU.subtract),
                lambda: dve.tensor_scalar(lohi_i[:, 0:1], lohi[:, 3:4], 2.0 * SHORTEST, None, ALU.max),
                lambda: dve.tensor_scalar(lohi_i[:, 1:2], lohi_i[:, 0:1], 1, None, ALU.arith_shift_right),
            )
            dve.tensor_copy(lohi[:, 3:4], lohi_i[:, 1:2]).then_inc(span_col, 1)
            dve.wait_ge(pe_edge, 4 + 2 * EB)
            dve.tensor_copy(span_lo[:, 0:NT], bank[6][0:1, 0:NT])
            dve.tensor_copy(span_n[:, 0:NT], bank[6][0:1, 32:32 + NT]).then_inc(span_rdy, 1)

            dve.wait_ge(wb_h, 1)
            dve.tensor_tensor(wbl[:, :, :, :], wraw[:, :, :, :], wbh[:, :, :, :], ALU.subtract).then_inc(wb_l, 1)
            dve.wait_ge(ld_x, 16 * 5)
            statistics(P, FULL + 1, lambda k: xall[:, k, :])

            def normalise_x(t, par, wait=True):
                if wait:
                    dve.wait_ge(xp_t, t - 1)
                at = bass.ds(t, 1)
                dve.tensor_scalar(xnorm[:, par, :], xall[:, at, :].rearrange("p a d -> p (a d)"),
                                  mv[:, at, 0], rs[:, at], ALU.subtract, ALU.mult).then_inc(xhat_rdy, 1)

            def low_part(t, par):
                dve.wait_ge(xp_h, t + 1)
                dve.tensor_tensor(xpl[:, par, :, :].rearrange("p c n -> p (c n)"), bank_tp[par][:, 0:D],
                                  xph[:, par, :, :].rearrange("p c n -> p (c n)"), ALU.subtract).then_inc(xp_l, 1)

            def copy_y(t, par, u):
                dve.wait_ge(y_mm, t * 4 + u + 1)
                dve.tensor_copy(ybuf[:, par, 4:8, u // 2, :],
                                bank_y[u][:, :].rearrange("p (r g) -> p r g", g=P)).then_inc(y_ev_v, 1)

            normalise_x(0, 0, False)
            normalise_x(1, 1, False)
            low_part(0, 0)
            normalise_x(2, 0)
            low_part(1, 1)
            copy_y(0, 0, 1)
            copy_y(0, 0, 3)
            with dve.Fori(0, FULL // 2 - 1) as i:
                for par in range(2):
                    t = i * 2 + 2 + par
                    normalise_x(t + 1, 1 - par)
                    low_part(t, par)
                    dve.wait_ge(y_st[1 - par], i * 16 + 16)
                    copy_y(t - 1, 1 - par, 1)
                    copy_y(t - 1, 1 - par, 3)
            low_part(FULL, 0)
            dve.wait_ge(y_st[1], 16 + (FULL // 2 - 1) * 16)
            copy_y(FULL - 1, 1, 1)
            copy_y(FULL - 1, 1, 3)
            dve.wait_ge(y_st[0], (FULL // 2) * 16)
            copy_y(FULL, 0, 1)
            copy_y(FULL, 0, 3)

            dve.wait_ge(y_st[0], 16 * (FULL // 2) + 32)
            dve.wait_ge(y_st[1], 16 + 16 * (FULL // 2))
            dve.memset(xth[:, :, :].bitcast(F32), 0.0)
            dve.memset(xtl[:, :, :].bitcast(F32), 0.0).then_inc(early_done, 1)
            for e in range(X):
                dve.wait_ge(w_h, 2 * e + 1)
                dve.tensor_tensor(w1l[:, :, e, :], w_stage[:, 0, :].rearrange("p (c h) -> p c h", c=DC),
                                  w1h[:, :, e, :], ALU.subtract).then_inc(w_l, 1)
                dve.wait_ge(w_h, 2 * e + 2)
                dve.tensor_tensor(w2l[:, :, e, :], w_stage[:, 1, :].rearrange("p (c d) -> p c d", c=HC),
                                  w2h[:, :, e, :], ALU.subtract).then_inc(w_l, 1)

            pair = dve.alloc_register("dve_pair")
            ecol = dve.alloc_register("dve_col")
            dve.reg_mov(pair, 0)

            def match_part(g, k, part, parts):
                if part == 0:
                    dve.reg_load(ecol, span_lo[0:1, bass.ds(g * GT + k, 1)])
                    dve.wait_ge(m_rdy, dve.snap(pair, min_val=0, max_val=NEVER * NT) * 2 + 2)
                    dve.tensor_scalar(iota_s[:, :], iota[:, :], starts[:, bass.ds(g * GT + k, 1)], None,
                                      ALU.add).then_inc(iota_rdy, 1)
                    dve.wait_ge(iota_rdy, g * GT + k + 1)
                    dve.sem_inc(dve_go, 1)
                n = part_of(dve, g, k, part, parts)
                with dve.Fori(0, n):
                    p = dve.snap(pair, min_val=0, max_val=NEVER * NT)
                    c = dve.snap(ecol, min_val=0, max_val=ECP - 2)
                    for ab in range(2):
                        if ab == 0:
                            dve.wait_ge(a_used, p + 1)
                        else:
                            dve.wait_ge(pair_used, p + RING)
                        dve.tensor_scalar(m_ab[:, ab, :], iota_s[:, :], dst_t[:, bass.ds(c + ab, 1)],
                                          norm_t[:, bass.ds(c + ab, 1)], ALU.is_equal, ALU.mult).then_inc(m_rdy, 1)
                    dve.reg_add(pair, pair, 1)
                    dve.reg_add(ecol, ecol, 2)

            def both_statistics(g, par, tiles):
                dve.wait_ge(x1_rdy, g * GT + tiles)
                statistics(TN, tiles, lambda k: x1[0:TN, par, k, :], 1.0 + EPS, EPS * EPS)

            def normalise(g, par, tiles):
                each(tiles, lambda k: centre(TN, k, x1[0:TN, par, k, :], xz[0:TN, k, :]))().then_inc(z_rdy, 1)

            def activations(g, par, first, tiles):
                last_k = min(first + 2, tiles)
                dve.wait_ge(t_made, g * 4 + first // 2 + 1)
                for k in range(first, last_k):
                    for c in range(DC):
                        at = (k - first) * D + c * P
                        last = dve.tensor_scalar(xtf[:, c, k * SLOT:k * SLOT + TN], bank_t[:, at:at + TN],
                                                 gam[:, c:c + 1], bet[:, c:c + 1], ALU.mult, ALU.add)
                last.then_inc(t_read, 1)
                dve.wait_ge(t_read, g * 4 + first // 2 + 1)
                for k in range(first, last_k):
                    f = slice(k * SLOT, k * SLOT + TN)
                    last = dve.tensor_copy(xth[:, par, :, f], xtf[:, :, f])
                chain(lambda: last)
                for k in range(first, last_k):
                    f = slice(k * SLOT, k * SLOT + TN)
                    dve.tensor_tensor(xtl[:, par, :, f], xtf[:, :, f], xth[:, par, :, f], ALU.subtract).then_inc(xt_rdy, 1)

            def rank(g, tiles):
                use = (tiles + 1) // 2
                dve.wait_ge(t_made, g * 4 + use + 1)
                for k in range(tiles):
                    last = dve.tensor_tensor(logit[0:TN, k, :], bank_t[0:TN, k * X:(k + 1) * X], br_s[0:TN, :], ALU.add)
                last.then_inc(t_read, 1)
                dve.wait_ge(t_read, g * 4 + use + 1)
                dve.sem_inc(dve_go, 1)
                chain(
                    each(tiles, lambda k: dve.max(mx8[0:TN, k, :], logit[0:TN, k, :])),
                    each(tiles, lambda k: dve.max_index(ix8[0:TN, k, :], mx8[0:TN, k, :], logit[0:TN, k, :])),
                )
                dve.tensor_tensor(dlt[0:TN, 0:tiles], mx8[0:TN, 0:tiles, 0], mx8[0:TN, 0:tiles, 1],
                                  ALU.subtract).then_inc(dlt_rdy, 1)
                dve.tensor_copy(ixf[0:TN, 0:tiles, :], ix8[0:TN, 0:tiles, :])

            def weigh(g, tiles):
                dve.wait_ge(tnh_rdy, g + 1)
                if not (isinstance(g, int) and g == 0):
                    dve.wait_ge(y2_add, g * (GT * X) + GT)
                chain(
                    lambda: (dve.tensor_scalar(w12[0:TN, 0, 0:tiles], tnh[0:TN, 0:tiles], 0.5, 0.5, ALU.mult, ALU.add),
                             dve.tensor_scalar(w12[0:TN, 1, 0:tiles], tnh[0:TN, 0:tiles], -0.5, 0.5, ALU.mult, ALU.add))[1],
                    lambda: (each(tiles, lambda k: dve.tensor_scalar(
                        wfull[0:TN, k, :], iota8[0:TN, :], ixf[0:TN, k, 0:1], w12[0:TN, 0, k:k + 1],
                        ALU.is_equal, ALU.mult))(),
                        each(tiles, lambda k: dve.tensor_scalar(
                            logit[0:TN, k, :], iota8[0:TN, :], ixf[0:TN, k, 1:2], w12[0:TN, 1, k:k + 1],
                            ALU.is_equal, ALU.mult))())[1],
                )
                dve.tensor_tensor(wfull[0:TN, 0:tiles, :], wfull[0:TN, 0:tiles, :], logit[0:TN, 0:tiles, :],
                                  ALU.add).then_inc(wf_rdy, 1)

            def take_weights(g, tiles):
                use = (tiles + 1) // 2 + 1
                dve.wait_ge(t_made, g * 4 + use + 1)
                for k in range(tiles):
                    last = dve.tensor_copy(wft[:, k * SLOT:k * SLOT + TN], bank_t[0:X, k * SLOT:k * SLOT + TN])
                last.then_inc(wft_rdy, 1)
                dve.wait_ge(wft_rdy, g + 1)
                dve.sem_inc(t_read, 1)

            def add_bias2(g, par, tiles):
                for k in range(tiles):
                    dve.wait_ge(b_mm, g * GT + k + 1)
                    dve.wait_ge(y2_add, g * (GT * X) + GT + k + 1)
                    dve.tensor_tensor(x1[0:TN, par, k, :], bank_o[k][0:TN, 0:D], x1[0:TN, par, k, :],
                                      ALU.add).then_inc(b_add, 1)

            def low_parts(g, e, tiles):
                cols = tiles * SLOT
                for hc in range(HC):
                    dve.wait_ge(h_act, g * (X * HC) + e * HC + hc + 1)
                    dve.tensor_tensor(hl[:, e % 2, hc, 0:cols], act_h[:, hc % 2, 0:cols], hh[:, e % 2, hc, 0:cols],
                                      ALU.subtract).then_inc(h_split, 1)

            def add(g, par, e, tiles):
                for k in range(tiles):
                    dve.wait_ge(y2_mm, g * (GT * X) + e * tiles + k + 1 + GT)
                    if e == 1:
                        dve.wait_ge(b_add, g * GT + k + 1)
                    elif e:
                        dve.wait_ge(y2_add, GT + g * (GT * X) + (e - 1) * tiles + k + 1)
                    dve.scalar_tensor_tensor(out=x1[0:TN, par, k, :], in0=bank_o[k][0:TN, 0:D],
                                             scalar=wfull[0:TN, k, e:e + 1], in1=x1[0:TN, par, k, :],
                                             op0=ALU.mult, op1=ALU.add).then_inc(y2_add, 1)

            def experts(g, par, tiles, ahead):
                def match(e, place):
                    k, part = PARTS.get((e, place), (GT, 0))
                    if k < ahead:
                        match_part(g + 1, k, part, PIECES[k])

                match(0, "up")
                for e in range(X):
                    if e == 1:
                        add_bias2(g, par, tiles)
                    if e == X - 2 and ahead:
                        activations(g + 1, 1 - par, 0, ahead)
                    if e == X - 1 and ahead:
                        rank(g + 1, ahead)
                    if e + 1 < X:
                        low_parts(g, e + 1, tiles)
                    elif ahead:
                        low_parts(g + 1, 0, ahead)
                    match(e, "down")
                    match(e + 1, "up")
                    if e == 0:
                        take_weights(g, tiles)
                    if e == X - 4 and ahead:
                        both_statistics(g + 1, 1 - par, ahead)
                    if e == X - 3 and ahead:
                        normalise(g + 1, 1 - par, ahead)
                    if e == X - 2 and ahead > 2:
                        activations(g + 1, 1 - par, 2, ahead)
                    add(g, par, e, tiles)
                if ahead:
                    weigh(g + 1, ahead)

            for k in range(GT):
                match_part(0, k, 0, 1)
            both_statistics(0, 0, GT)
            normalise(0, 0, GT)
            activations(0, 0, 0, GT)
            activations(0, 0, 2, GT)
            rank(0, GT)
            low_parts(0, 0, GT)
            weigh(0, GT)
            with dve.Fori(0, (NG - 2) // 2) as i:
                for par in range(2):
                    experts(i * 2 + par, par, GT, GT)
            experts(NG - 2, 0, GT, GT)
            experts(NG - 1, 1, GT, 1)
            experts(NG, 0, 1, 0)


def kernel(x, src, dst, edge_type_8, edge_weight, L0_gnn_weight, L0_ffn_gamma, L0_ffn_beta, L0_ffn_Wr, L0_ffn_br,
           L0_ffn_W1, L0_ffn_b1, L0_ffn_W2, L0_ffn_b2):
    from concourse import bacc
    from concourse.bass_utils import run_bass_kernel_spmd

    first_nodes = TN * np.array(ORDER)
    ins = {
        "x": x, "src": src, "dst": dst, "rel": edge_type_8, "norm": edge_weight,
        "gnn_w": np.asarray(L0_gnn_weight).reshape(R, NB * SB * SB), "gamma": L0_ffn_gamma, "beta": L0_ffn_beta,
        "wr": L0_ffn_Wr, "br": L0_ffn_br, "w1": L0_ffn_W1, "b1": L0_ffn_b1, "w2": L0_ffn_W2, "b2": L0_ffn_b2,
        "starts_f": first_nodes.astype(np.float32), "starts_i": first_nodes.astype(np.int32).reshape(1, NT),
    }
    ins = {name: np.ascontiguousarray(a) for name, a in ins.items()}
    nc = bacc.Bacc("TRN2", target_bir_lowering=False, num_devices=1)
    aps = {name: nc.dram_tensor(f"in_{name}", a.shape, mybir.dt.from_np(a.dtype), kind="ExternalInput").ap()
           for name, a in ins.items()}
    out = nc.dram_tensor("out_x", (N, D), F32, kind="ExternalOutput").ap()
    build_program(nc, out=out, **aps)
    r = run_bass_kernel_spmd(nc, [{f"in_{name}": a for name, a in ins.items()}], core_ids=[0])
    return r.results[0]["out_x"]
```

```python
from contextlib import ExitStack

import numpy as np

import concourse.bass as bass
from concourse import mybir

F32 = mybir.dt.float32
F32R = mybir.dt.float32r
I32 = mybir.dt.int32
U32 = mybir.dt.uint32
ALU = mybir.AluOpType
ACT = mybir.ActivationFunctionType
AX = mybir.AxisListType

P = 128
N, D = 3125, 256
E = 50000
R = 8
NB = 8
SB = D // NB
X, H = 8, 512
DC, HC = D // P, H // P
EPS = 1e-5

TN = 125
NT = N // TN
GT = 3
NG = NT // GT
SLOT = P
COLS = GT * SLOT
FULL = N // P
REST = N - FULL * P
YB = 4
HALVES = 2 * X
STAGES = 6
EC = (E + P - 1) // P
EB = (EC + P - 1) // P
QC = 4
LEAST = (4, 3, 3)
ECP = EC + QC * max(LEAST)
RING = 4
LAG = 2
THIRD = 21846
NEVER = 4096
FAR = 1.0e4

ORDER = [22, 23, 21, 0, 20, 19, 1, 18, 17, 2, 16, 15, 3, 14, 13, 4, 12, 11, 5, 10, 9, 6, 8, 7, 24]
PIECES = (4, 3, 3)
PARTS = {(0, "up"): (0, 0), (0, "down"): (0, 1), (1, "up"): (0, 2), (1, "down"): (0, 3),
         (2, "up"): (1, 0), (2, "down"): (1, 1), (3, "up"): (1, 2),
         (3, "down"): (2, 0), (4, "up"): (2, 1), (4, "down"): (2, 2)}
assert all(a <= b for a, b in zip(PIECES, LEAST)) and ECP <= EB * P and len(PARTS) % 2 == 0
assert NT * TN == N and NG * GT + 1 == NT and sorted(ORDER) == list(range(NT))


def build_program(nc, x, src, dst, rel, norm, gnn_w, gamma, beta, wr, br, w1, b1, w2, b2,
                  starts_f, starts_i, least, out):
    y = nc.dram_tensor("y_rows", [N * R, D], F32).ap()
    y_nodes = y.rearrange("(n r) d -> n (r d)", r=R)

    top = ExitStack()
    with top:
        def sb(stack, name, shape, dt=F32):
            return stack.enter_context(nc.sbuf_tensor(name, shape, dt))

        def sem(name):
            return top.enter_context(nc.semaphore(name))

        bank = [top.enter_context(nc.psum_tensor(f"bank{i}", [P, 512], F32)) for i in range(8)]

        row_t = sb(top, "row_t", [P, ECP], I32)
        dst_t = sb(top, "dst_t", [P, ECP])
        norm_t = sb(top, "norm_t", [P, ECP])
        ident = sb(top, "ident", [P, P])
        iota = sb(top, "iota", [P, TN])
        starts = sb(top, "starts", [P, NT])
        starts_r = sb(top, "starts_r", [1, 32], I32)
        span_lo = sb(top, "span_lo", [1, 32], I32)
        span_n = sb(top, "span_n", [1, 32], I32)
        turns_s = sb(top, "turns_s", [1, 2], I32)
        gam = sb(top, "gam", [P, DC])
        bet = sb(top, "bet", [P, DC])
        wr_s = sb(top, "wr_s", [P, DC, X])
        br_s = sb(top, "br_s", [P, X])
        b1_s = sb(top, "b1_s", [P, X, HC])
        b2_s = sb(top, "b2_s", [X, D])
        iota8 = sb(top, "iota8", [P, X])
        zero_r = sb(top, "zero_r", [P, TN + 1], F32R)
        mv = sb(top, "mv", [P, FULL + 1, 2])
        rs = sb(top, "rs", [P, FULL + 1])
        rt = sb(top, "rt", [P, FULL + 1])
        ve = sb(top, "ve", [P, FULL + 1])

        with ExitStack() as staging:
            w_stage = sb(staging, "w_stage", [P, STAGES, DC * H])
        hh = sb(top, "hh", [P, 2, HC, COLS], F32R)
        with ExitStack() as staging:
            hidden = sb(staging, "hidden", [P, 2, HC, COLS])
        hl = sb(top, "hl", [P, 2, HC, COLS], F32R)

        with ExitStack() as early:
            xall = sb(early, "xall", [P, FULL + 1, D])
            stat_x = sb(early, "stat_x", [P, FULL + 1, 6])
            xnorm = sb(early, "xnorm", [P, 2, D])
            wbh = sb(early, "wbh", [P, DC, R, P], F32R)
            wbl = sb(early, "wbl", [P, DC, R, P], F32R)
            xph = sb(early, "xph", [P, 2, DC, P], F32R)
            xpl = sb(early, "xpl", [P, 2, DC, P], F32R)
            ybuf = sb(early, "ybuf", [P, YB, R, DC, P])
            wraw = sb(early, "wraw", [P, DC, R, P])
            e_src = sb(early, "e_src", [P, EB, P], I32)
            e_dst = sb(early, "e_dst", [P, EB, P], I32)
            e_rel = sb(early, "e_rel", [P, EB, P], I32)
            e_norm = sb(early, "e_norm", [P, EB, P])
            rowf = sb(early, "rowf", [P, EB, P])
            dstf = sb(early, "dstf", [P, EB, P])
            diag = sb(early, "diag", [P, 2, P])
            iota_t = sb(early, "iota_t", [NT, EC])
            hit = sb(early, "hit", [NT, EC])
            hit2 = sb(early, "hit2", [NT, EC])
            ones = sb(early, "ones", [P, NT])
            mnmx = sb(early, "mnmx", [P, 2, EB])
            ends = sb(early, "ends", [NT, 2])
            least_s = sb(early, "least_s", [NT, 1])
            lohi = sb(early, "lohi", [NT, 4])
            lohi_i = sb(early, "lohi_i", [NT, 2], I32)

        w1h = sb(top, "w1h", [P, DC, X, H], F32R)
        w1l = sb(top, "w1l", [P, DC, X, H], F32R)
        w2h = sb(top, "w2h", [P, HC, X, D], F32R)
        w2l = sb(top, "w2l", [P, HC, X, D], F32R)
        gath = sb(top, "gath", [P, QC * RING, D])
        idx = sb(top, "idx", [P, QC * RING], I32)
        m_s = sb(top, "m_s", [P, 2 * QC, TN])
        iota_s = sb(top, "iota_s", [P, TN])
        xtf = sb(top, "xtf", [P, DC, COLS])
        xth = sb(top, "xth", [P, 2, DC, COLS], F32R)
        xtl = sb(top, "xtl", [P, 2, DC, COLS], F32R)
        xz = sb(top, "xz", [P, GT, D])
        x1 = sb(top, "x1", [P, 2, GT, D])
        stat = sb(top, "stat", [P, GT, 6])
        logit = sb(top, "logit", [P, GT, X])
        mx8 = sb(top, "mx8", [P, GT, X])
        ix8 = sb(top, "ix8", [P, GT, X], U32)
        ixf = sb(top, "ixf", [P, GT, X])
        dlt = sb(top, "dlt", [P, GT])
        tnh = sb(top, "tnh", [P, GT])
        w12 = sb(top, "w12", [P, 2, GT])
        wfull = sb(top, "wfull", [P, GT, X])
        wft = xtf[0:X, :, :].rearrange("p c n -> p (c n)")

        ld_edge = sem("ld_edge")
        ld_x = [sem(f"ld_x{i}") for i in range(5)]
        ld_wb = sem("ld_wb")
        ld_small = sem("ld_small")
        ld_w = [sem(f"ld_w{i}") for i in range(STAGES)]
        pool_const = sem("pool_const")
        fill = sem("fill")
        edge_f = sem("edge_f")
        diag_rdy = sem("diag_rdy")
        pe_edge = sem("pe_edge")
        span_col = sem("span_col")
        span_rdy = sem("span_rdy")
        dve_seq = sem("dve_seq")
        dve_go = sem("dve_go")
        xhat_rdy = sem("xhat_rdy")
        wb_h = sem("wb_h")
        wb_l = sem("wb_l")
        xp_t = sem("xp_t")
        xp_h = sem("xp_h")
        xp_l = sem("xp_l")
        y_mm = sem("y_mm")
        y_ev_a = sem("y_ev_a")
        y_ev_v = sem("y_ev_v")
        y_st = [sem(f"y_st{i}") for i in range(YB)]
        w_h = sem("w_h")
        w_l = sem("w_l")
        table_rdy = sem("table_rdy")
        early_done = sem("early_done")
        idx_rdy = sem("idx_rdy")
        land = [sem(f"land{i}") for i in range(RING)]
        landed = sem("landed")
        m_used = sem("m_used")
        m_rdy = sem("m_rdy")
        iota_rdy = sem("iota_rdy")
        ld_xin = [sem(f"ld_xin{i}") for i in range(GT)]
        acc_rdy = sem("acc_rdy")
        x1_rdy = sem("x1_rdy")
        z_rdy = sem("z_rdy")
        t_made = sem("t_made")
        t_read = sem("t_read")
        xt_rdy = sem("xt_rdy")
        wf_rdy = sem("wf_rdy")
        wft_rdy = sem("wft_rdy")
        dlt_rdy = sem("dlt_rdy")
        tnh_rdy = sem("tnh_rdy")
        b_mm = sem("b_mm")
        b_add = sem("b_add")
        h_mm = sem("h_mm")
        h_act = sem("h_act")
        h_split = sem("h_split")
        y2_mm = sem("y2_mm")
        y2_add = sem("y2_add")
        st_out = [sem(f"st_out{i}") for i in range(GT)]

        bank_y, bank_tp = bank[0:4], bank[4:6]
        bank_h, bank_o, bank_acc, bank_t = bank[0:3], bank[3:6], bank[6], bank[7]

        gnn_v = gnn_w.rearrange("r (b i o) -> b i r o", b=NB, i=SB)
        w1_v = w1.rearrange("e (c p) h -> e p c h", p=P)
        w2_v = w2.rearrange("e (c p) d -> e p c d", p=P)
        n_small = 10
        full_rows = E // P
        rest_e = E - full_rows * P
        eb_full = full_rows // P
        eb_rest = full_rows - eb_full * P

        def part_of(engine, g, k, part, parts):
            n = engine.value_load(span_n[0:1, bass.ds(g * GT + k, 1)], min_val=min(LEAST), max_val=NEVER)
            return n if parts == 1 else (n + part) // 4 if parts == 4 else ((n + part) * THIRD) // (1 << 16)

        block = top.enter_context(nc.Block())

        def hidden_bank(e, hc, tiles):
            if tiles == GT or e == 0:
                return bank_h[(e + hc) % 3], 2 if e == 0 and hc < 2 else 3
            five = [*bank_h, *bank_o[1:3]]
            return five[(e * HC + hc) % 5], 2 if e == 1 else 5

        def y_stored(engine):
            for i in range(YB):
                engine.wait_ge(y_st[i], 16 * (FULL // YB) + (32 if i == FULL % YB else 0))

        def half(h):
            e, stage = h // 2, w_stage[:, h % STAGES, :]
            if h % 2 == 0:
                return w1_v[e], stage.rearrange("p (c h) -> p c h", c=DC), w1h[:, :, e, :], w1l[:, :, e, :]
            return w2_v[e], stage.rearrange("p (c d) -> p c d", c=HC), w2h[:, :, e, :], w2l[:, :, e, :]

        @block.sync
        def _(sp):
            for k in range(GT):
                sp.sem_inc(st_out[k], 16)
            arrays = ((src, e_src), (dst, e_dst), (rel, e_rel), (norm, e_norm))
            rows = [a[0:full_rows * P].rearrange("(t p) -> t p", p=P) for a, _ in arrays]
            for r, (a, t) in zip(rows, arrays):
                sp.dma_start(t[:, 0:eb_full, :],
                             r[0:eb_full * P].rearrange("(b t) p -> t b p", t=P)).then_inc(ld_edge, 16)
            sp.wait_ge(fill, 2)
            for r, (a, t) in zip(rows, arrays):
                sp.dma_start(t[0:eb_rest, eb_full, :], r[eb_full * P:full_rows]).then_inc(ld_edge, 16)
                sp.dma_start(t[eb_rest:eb_rest + 1, eb_full, 0:rest_e],
                             a[full_rows * P:E].rearrange("(a n) -> a n", a=1)).then_inc(ld_edge, 16)
            q = FULL // 4
            for c in range(4):
                sp.dma_start(xall[:, c * q:(c + 1) * q, :],
                             x[c * q * P:(c + 1) * q * P, :].rearrange("(t p) d -> p t d", p=P)).then_inc(ld_x[c], 16)
            sp.dma_start(xall[0:REST, FULL, :], x[FULL * P:N, :]).then_inc(ld_x[4], 16)

            def store_y(t, j):
                sp.wait_ge(y_ev_a, t * 2 + 2)
                sp.wait_ge(y_ev_v, t * 2 + 2)
                sp.dma_start(y_nodes[bass.ds(t * P, P), :],
                             ybuf[:, j, :, :, :].rearrange("p r c g -> p (r c g)")).then_inc(y_st[j], 16)

            def load_half(h):
                there, stage, _, _ = half(h)
                sp.dma_start(stage, there).then_inc(ld_w[h % STAGES], 16)

            for h in range(STAGES):
                load_half(h)
            for t in range(YB):
                store_y(t, t)
            with sp.Fori(1, FULL // YB) as i:
                for j in range(YB):
                    store_y(i * YB + j, j)
            sp.wait_ge(y_ev_a, FULL * 2 + 2)
            sp.wait_ge(y_ev_v, FULL * 2 + 2)
            yb = ybuf[:, FULL % YB, :, :, :].rearrange("p r c g -> p (r c g)")
            k = REST // 16 * 16
            sp.dma_start(y_nodes[FULL * P:FULL * P + k, :], yb[0:k, :]).then_inc(y_st[FULL % YB], 16)
            sp.dma_start(y_nodes[FULL * P + k:N, :], yb[k:REST, :]).then_inc(y_st[FULL % YB], 16)

            def load_xin(g, k):
                start = sp.value_load(starts_r[0:1, bass.ds(g * GT + k, 1)], min_val=0, max_val=N - TN)
                sp.dma_start(xz[0:TN, k, :], x[bass.ds(start, TN), :]).then_inc(ld_xin[k], 16)

            y_stored(sp)
            sp.wait_ge(ld_small, 16 * n_small)
            for k in range(GT):
                load_xin(0, k)
            for h in range(STAGES, HALVES):
                sp.wait_ge(w_l, h - STAGES + 1)
                load_half(h)

            def store_out(g, par, tiles):
                for k in range(tiles):
                    sp.wait_ge(y2_add, GT + g * (GT * X) + (X - 1) * tiles + k + 1)
                    start = sp.value_load(starts_r[0:1, bass.ds(g * GT + k, 1)], min_val=0, max_val=N - TN)
                    sp.dma_start(out[bass.ds(start, TN), :], x1[0:TN, par, k, :]).then_inc(st_out[k], 16)

            def load_group(g, tiles):
                sp.wait_ge(t_made, g * 4 - 2)
                for k in range(tiles):
                    load_xin(g, k)

            load_group(1, GT)
            with sp.Fori(0, (NG - 2) // 2) as i:
                for par in range(2):
                    load_group(i * 2 + par + 2, GT)
                    store_out(i * 2 + par, par, GT)
            load_group(NG, 1)
            for g in range(NG - 2, NG):
                store_out(g, g % 2, GT)
            store_out(NG, NG % 2, 1)
            sp.wait_ge(st_out[0], 16 * (NG + 2))
            for k in range(1, GT):
                sp.wait_ge(st_out[k], 16 * (NG + 1))

        @block.gpsimd
        def _(pool):
            pool.memset(ident[:, :], 0.0).then_inc(pool_const, 1)
            pool.wait_ge(pool_const, 1)
            pool.affine_select(out=ident[:, :], in_=ident[:, :], compare_op=ALU.not_equal, fill=1.0,
                               base=0, pattern=[[-1, P]], channel_multiplier=1).then_inc(pool_const, 1)
            pool.iota(iota[:, :], pattern=[[1, TN]], base=0, channel_multiplier=0,
                      allow_small_or_imprecise_dtypes=True).then_inc(pool_const, 1)
            pool.iota(iota8[:, :], pattern=[[1, X]], base=0, channel_multiplier=0,
                      allow_small_or_imprecise_dtypes=True).then_inc(pool_const, 1)
            pool.iota(iota_t[:, :], pattern=[[1, EC]], base=0, channel_multiplier=0,
                      allow_small_or_imprecise_dtypes=True).then_inc(pool_const, 1)
            pool.wait_ge(wb_h, 1)
            pool.tensor_tensor(wbl[:, :, :, :], wraw[:, :, :, :], wbh[:, :, :, :], ALU.subtract).then_inc(wb_l, 1)
            pool.wait_ge(table_rdy, 1)
            pool.wait_ge(span_rdy, 1)
            turns = pool.value_load(turns_s[0:1, 1:2], min_val=NT * min(LEAST) // RING, max_val=NEVER * NT)
            col = pool.alloc_register("col")
            left = pool.alloc_register("left")
            at = pool.alloc_register("at")
            pool.reg_mov(at, 0)
            pool.reg_load(col, span_lo[0:1, 0:1])
            pool.reg_load(left, span_n[0:1, 0:1])
            y_stored(pool)

            def gather_batch(turn, j, first=False):
                if not (isinstance(turn, int) and turn == 0):
                    pool.wait_ge(m_used, (turn * RING + (j + 2 - RING)) * QC + 1)
                c = pool.snap(col, min_val=0, max_val=ECP - QC)
                own = slice(QC * j, QC * j + QC)
                pool.tensor_copy(idx[:, own], row_t[:, bass.ds(c, QC)]).then_inc(idx_rdy, 1)
                pool.reg_add(col, col, QC)
                pool.reg_sub(left, left, 1)
                with pool.If_eq(left, 0):
                    pool.reg_add(at, at, 1)
                    a = pool.snap(at, min_val=0, max_val=NT)
                    pool.reg_load(col, span_lo[0:1, bass.ds(a, 1)])
                    pool.reg_load(left, span_n[0:1, bass.ds(a, 1)])
                pool.wait_ge(idx_rdy, turn * RING + j + 1)
                if not first:
                    pool.wait_ge(land[(j - LAG) % RING], (turn + (1 if j >= LAG else 0)) * (16 * QC))
                pool.sem_inc(landed, 1)
                for s in range(QC * j, QC * j + QC):
                    pool.indirect_dma_start(
                        out=gath[:, s, :], out_offset=None, in_=y,
                        in_offset=bass.IndirectOffsetOnAxis(ap=idx[:, s:s + 1], axis=0),
                    ).then_inc(land[j], 16)

            for j in range(RING):
                gather_batch(0, j, j < LAG)
            with pool.Fori(1, turns) as turn:
                for j in range(RING):
                    gather_batch(turn, j)
            for j in range(LAG):
                pool.wait_ge(land[RING - LAG + j], turns * (16 * QC))
                pool.sem_inc(landed, 1)
            for j in range(RING):
                pool.wait_ge(land[j], turns * (16 * QC))

        @block.tensor
        def _(pe):
            def split_mm(outp, stat_h, stat_l, mov_h, mov_l, start, stop):
                pe.matmul(outp, stat_h, mov_h, start=start, stop=False)
                pe.matmul(outp, stat_h, mov_l, start=False, stop=False)
                return pe.matmul(outp, stat_l, mov_h, start=False, stop=stop)

            pe.sem_inc(y2_mm, GT)
            pe.sem_inc(m_used, QC + 1)
            pe.wait_ge(pool_const, 2)
            pe.wait_ge(edge_f, 3)
            for b, t in enumerate((rowf, dstf, e_norm)):
                for k in range(EB):
                    last = pe.transpose(bank[b][:, k * P:(k + 1) * P], t[:, k, :], ident[:, :])
                last.then_inc(pe_edge, 1)
            for i in range(2 * EB):
                pe.wait_ge(diag_rdy, i + 1)
                pe.matmul(bank[6 + i // EB][0:NT, (i % EB) * P:(i % EB + 1) * P], ones[:, :],
                          diag[:, i % 2, :], start=True, stop=True).then_inc(pe_edge, 1)

            def make_y(t, par):
                pe.wait_ge(xhat_rdy, t + 1)
                if not (isinstance(t, int) and t < 2):
                    pe.wait_ge(xp_l, t - 1)
                for c in range(DC):
                    last = pe.transpose(bank_tp[par][:, c * P:(c + 1) * P],
                                        xnorm[:, par, c * P:(c + 1) * P], ident[:, :])
                last.then_inc(xp_t, 1)

            def mul_y(t, par):
                pe.wait_ge(xp_l, t + 1)
                for u in range(4):
                    c, half = u // 2, u % 2
                    if not (isinstance(t, int) and t == 0):
                        pe.wait_ge(y_ev_v if half else y_ev_a, t * 2 + c - 1)
                    split_mm(bank_y[u][:, :], xph[:, par, c, :], xpl[:, par, c, :],
                             wbh[:, c, 4 * half:4 * half + 4, :].rearrange("p r g -> p (r g)"),
                             wbl[:, c, 4 * half:4 * half + 4, :].rearrange("p r g -> p (r g)"),
                             True, True).then_inc(y_mm, 1)

            def tile_y(t, j):
                if not (isinstance(t, int) and t == FULL):
                    make_y(t + 1, (j + 1) % 2)
                mul_y(t, j % 2)

            make_y(0, 0)
            pe.wait_ge(wb_l, 1)
            pe.wait_ge(table_rdy, 1)
            for t in range(YB):
                tile_y(t, t)
            with pe.Fori(1, FULL // YB - 1) as i:
                for j in range(YB):
                    tile_y(i * YB + j, j)
            for t in range(FULL - YB, FULL + 1):
                tile_y(t, t % YB)
            pe.wait_ge(span_col, 1)
            for i in range(2):
                last = pe.transpose(bank[6][0:1, i * 32:i * 32 + NT], lohi[:, 2 + i:3 + i], ident[0:NT, 0:NT])
            last.then_inc(pe_edge, 1)

            batch = pe.alloc_register("pe_batch")
            slot = pe.alloc_register("pe_slot")
            pe.reg_mov(batch, 0)

            def sum_part(g, k, part, parts, m_set):
                if part == 0:
                    if not (isinstance(g, int) and g == 0 and k == 0):
                        pe.wait_ge(x1_rdy, g * GT + k)
                    pe.matmul(bank_acc[0:TN, 0:2], zero_r[:, 0:TN], zero_r[:, 0:2], start=True, stop=False,
                              skip_group_check=True)
                n = part_of(pe, g, k, part, parts)
                with pe.Fori(0, n):
                    b = pe.snap(batch, min_val=0, max_val=NEVER * NT)
                    pe.reg_alu(slot, batch, RING - 1, ALU.bitwise_and)
                    s = pe.snap(slot, min_val=0, max_val=RING - 1)
                    pe.wait_ge(landed, b + 1 + LAG)
                    for j in range(QC):
                        pe.wait_ge(m_rdy, b * QC + j + 1)
                        pe.matmul(bank_acc[0:TN, 0:D], m_s[:, m_set * QC + j, :],
                                  gath[:, bass.ds(s * QC + j, 1), :].rearrange("p a d -> p (a d)"),
                                  start=False, stop=False, skip_group_check=True).then_inc(m_used, 1)
                    pe.reg_add(batch, batch, 1)
                if part == parts - 1:
                    pe.wait_ge(ld_xin[k], g * 16 + 16)
                    pe.matmul(bank_acc[0:TN, 0:D], ident[0:TN, 0:TN], xz[0:TN, k, :], start=False, stop=True,
                              skip_group_check=True).then_inc(acc_rdy, 1)

            def t_free(g, i):
                if not (isinstance(g, int) and g * 4 + i == 0):
                    pe.wait_ge(t_read, g * 4 + i)

            def turn_over(g, first, tiles):
                pe.wait_ge(z_rdy, g + 1)
                t_free(g, first // 2)
                for k in range(first, min(first + 2, tiles)):
                    for c in range(DC):
                        at = (k - first) * D + c * P
                        last = pe.transpose(bank_t[:, at:at + TN], xz[0:TN, k, c * P:(c + 1) * P], ident[0:TN, 0:TN])
                last.then_inc(t_made, 1)

            def route(g, tiles):
                use = (tiles + 1) // 2
                t_free(g, use)
                pe.wait_ge(xt_rdy, g * GT + tiles)
                for k in range(tiles):
                    for c in range(DC):
                        last = pe.matmul(bank_t[0:TN, k * X:(k + 1) * X], xtf[:, c, k * SLOT:k * SLOT + TN],
                                         wr_s[:, c, :], start=(c == 0), stop=(c == DC - 1))
                last.then_inc(t_made, 1)

            def turn_weights(g, tiles):
                t_free(g, (tiles + 1) // 2 + 1)
                pe.wait_ge(wf_rdy, g + 1)
                for k in range(tiles):
                    last = pe.transpose(bank_t[0:X, k * SLOT:k * SLOT + TN], wfull[0:TN, k, :], ident[0:TN, 0:TN])
                last.then_inc(t_made, 1)

            def bias2(g, tiles):
                pe.wait_ge(wft_rdy, g + 1)
                for k in range(tiles):
                    pe.wait_ge(y2_add, g * (GT * X) + (GT + k + 1))
                    pe.matmul(bank_o[k][0:TN, 0:D], wft[:, k * SLOT:k * SLOT + TN], b2_s[:, :],
                              start=True, stop=True).then_inc(b_mm, 1)

            def up(g, par, e, tiles):
                cols = tiles * SLOT
                if e == 0:
                    pe.wait_ge(xt_rdy, g * GT + tiles)
                if e == 1 and tiles < GT:
                    pe.wait_ge(y2_add, g * (GT * X) + GT)
                for hc in range(HC):
                    bank_of, back = hidden_bank(e, hc, tiles)
                    if not (isinstance(g, int) and g * X * HC + e * HC + hc < back):
                        pe.wait_ge(h_act, g * (X * HC) + (e * HC + hc + 1 - back))
                    for c in range(DC):
                        f = slice(hc * P, (hc + 1) * P)
                        last = split_mm(bank_of[:, 0:cols], w1h[:, c, e, f], w1l[:, c, e, f],
                                        xth[:, par, c, 0:cols], xtl[:, par, c, 0:cols], c == 0, c == DC - 1)
                    last.then_inc(h_mm, 1)

            def down(g, e, tiles):
                pe.wait_ge(h_split, g * (X * HC) + e * HC + HC)
                for k in range(tiles):
                    if e == 1:
                        pe.wait_ge(b_add, g * GT + k + 1)
                    if not (isinstance(g, int) and g == 0 and e == 0):
                        if tiles == GT or e:
                            pe.wait_ge(y2_add, g * (GT * X) + (GT + (e - 1) * tiles + k + 1))
                        else:
                            pe.wait_ge(y2_add, g * (GT * X) + GT)
                    for hc in range(HC):
                        f = slice(k * SLOT, k * SLOT + TN)
                        last = split_mm(bank_o[k][0:TN, 0:D], hh[:, e % 2, hc, f], hl[:, e % 2, hc, f],
                                        w2h[:, hc, e, :], w2l[:, hc, e, :], hc == 0, hc == HC - 1)
                    last.then_inc(y2_mm, 1)

            def experts(g, par, tiles, ahead):
                for e in range(X):
                    for place in ("up", "down"):
                        k, part = PARTS.get((e, place), (GT, 0))
                        if k < ahead:
                            sum_part(g + 1, k, part, PIECES[k], list(PARTS).index((e, place)) % 2)
                        if place == "up":
                            if e == 1:
                                bias2(g, tiles)
                            if e == X - 2 and ahead:
                                turn_over(g + 1, 0, ahead)
                            if e == X - 1 and ahead:
                                route(g + 1, ahead)
                            if e + 1 < X:
                                up(g, par, e + 1, tiles)
                            elif ahead:
                                up(g + 1, 1 - par, 0, ahead)
                        else:
                            if e == 0:
                                turn_weights(g, tiles)
                            if e == X - 2 and ahead > 2:
                                turn_over(g + 1, 2, ahead)
                            down(g, e, tiles)

            pe.wait_ge(span_rdy, 1)
            pe.wait_ge(early_done, 1)
            for k in range(GT):
                sum_part(0, k, 0, 1, (GT - k) % 2)
            turn_over(0, 0, GT)
            turn_over(0, 2, GT)
            route(0, GT)
            pe.wait_ge(w_l, 2 * X)
            up(0, 0, 0, GT)
            with pe.Fori(0, (NG - 2) // 2) as i:
                for par in range(2):
                    experts(i * 2 + par, par, GT, GT)
            experts(NG - 2, 0, GT, GT)
            experts(NG - 1, 1, GT, 1)
            experts(NG, 0, 1, 0)

        @block.scalar
        def _(act):
            act.dma_start(starts_r[:, 0:NT], starts_i).then_inc(ld_small, 16)
            act.dma_start(starts[:, :], starts_f.partition_broadcast(P)).then_inc(ld_small, 16)
            act.wait_ge(fill, 1)
            for b in range(NB):
                c, q = b * SB // P, b * SB % P
                act.dma_start(wraw[q:q + SB, c, :, q:q + SB], gnn_v[b]).then_inc(ld_wb, 16)
            act.dma_start(ends[:, 0:1], starts_f.rearrange("(n a) -> n a", a=1)).then_inc(ld_small, 16)
            act.dma_start(least_s[:, :], least.rearrange("(n a) -> n a", a=1)).then_inc(ld_small, 16)
            with nc.allow_non_contiguous_dma(reason="small parameters, once"):
                act.dma_start(gam[:, :], gamma.rearrange("(c p) -> p c", p=P)).then_inc(ld_small, 16)
                act.dma_start(bet[:, :], beta.rearrange("(c p) -> p c", p=P)).then_inc(ld_small, 16)
                act.dma_start(b1_s[:, :, :].rearrange("p e c -> p (e c)"),
                              b1.rearrange("e (c p) -> p (e c)", p=P)).then_inc(ld_small, 16)
            act.dma_start(wr_s[:, :, :], wr.rearrange("(c p) e -> p c e", p=P)).then_inc(ld_small, 16)
            act.dma_start(br_s[:, :], br.partition_broadcast(P)).then_inc(ld_small, 16)
            act.dma_start(b2_s[:, :], b2).then_inc(ld_small, 16)
            act.wait_ge(ld_wb, 16 * NB)
            act.activation(wbh[:, :, :, :], wraw[:, :, :, :], ACT.Copy).then_inc(wb_h, 1)
            act.wait_ge(pe_edge, 3)
            act.activation(row_t[:, 0:ECP], bank[0][:, 0:ECP], ACT.Copy)
            act.activation(dst_t[:, 0:ECP], bank[1][:, 0:ECP], ACT.Copy)
            act.activation(norm_t[:, 0:ECP], bank[2][:, 0:ECP], ACT.Copy).then_inc(table_rdy, 1)

            def part_of_y(t, par):
                act.wait_ge(xp_t, t + 1)
                act.activation(xph[:, par, :, :].rearrange("p c n -> p (c n)"), bank_tp[par][:, 0:D],
                               ACT.Copy).then_inc(xp_h, 1)

            def copy_y(t, j, u):
                act.wait_ge(y_mm, t * 4 + u + 1)
                act.activation(ybuf[:, j, 0:4, u // 2, :], bank_y[u][:, :].rearrange("p (r g) -> p r g", g=P),
                               ACT.Copy).then_inc(y_ev_a, 1)

            def tile_y(i, j):
                t = i * YB + j
                if not (isinstance(t, int) and t == FULL):
                    if not (isinstance(t, int) and t == 0):
                        act.wait_ge(y_mm, t * 4)
                    part_of_y(t + 1, (j + 1) % 2)
                if not (isinstance(t, int) and t < YB):
                    act.wait_ge(y_st[j], i * 16)
                copy_y(t, j, 0)
                copy_y(t, j, 2)

            part_of_y(0, 0)
            for t in range(YB):
                tile_y(0, t)
            with act.Fori(1, FULL // YB - 1) as i:
                for j in range(YB):
                    tile_y(i, j)
            for t in range(FULL - YB, FULL + 1):
                tile_y(t // YB, t % YB)

            y_stored(act)

            def high_part(h):
                _, stage, high, _ = half(h)
                act.wait_ge(ld_w[h % STAGES], 16 * (h // STAGES + 1))
                act.activation(high, stage, ACT.Copy).then_inc(w_h, 1)

            def take_x1(g, par, k):
                act.wait_ge(acc_rdy, g * GT + k + 1)
                if not (isinstance(g, int) and g < 2):
                    act.wait_ge(st_out[k], g * 16)
                act.activation(x1[0:TN, par, k, :], bank_acc[0:TN, 0:D], ACT.Copy).then_inc(x1_rdy, 1)

            def gelu(g, e, tiles):
                cols = tiles * SLOT
                if not (isinstance(g, int) and g == 0 and e < 2):
                    act.wait_ge(y2_mm, g * (GT * X) + ((e - 1) * tiles + GT if e else 0))
                for hc in range(HC):
                    bank_of, _ = hidden_bank(e, hc, tiles)
                    act.wait_ge(h_mm, g * (X * HC) + e * HC + hc + 1)
                    act.activation(hidden[:, e % 2, hc, 0:cols], bank_of[:, 0:cols], ACT.Gelu,
                                   bias=b1_s[:, e, hc:hc + 1])
                    act.activation(hh[:, e % 2, hc, 0:cols], bank_of[:, 0:cols], ACT.Gelu,
                                   bias=b1_s[:, e, hc:hc + 1]).then_inc(h_act, 1)

            def tanh_of_gap(g, tiles):
                act.wait_ge(dlt_rdy, g + 1)
                act.activation(tnh[0:TN, 0:tiles], dlt[0:TN, 0:tiles], ACT.Tanh, scale=0.5).then_inc(tnh_rdy, 1)

            def experts(g, par, tiles, ahead):
                def take(e, place):
                    k, part = PARTS.get((e, place), (GT, 0))
                    if k < ahead and part == PIECES[k] - 1:
                        take_x1(g + 1, 1 - par, k)

                for e in range(X):
                    take(e, "up")
                    if e + 1 < X:
                        gelu(g, e + 1, tiles)
                    elif ahead:
                        tanh_of_gap(g + 1, ahead)
                        gelu(g + 1, 0, ahead)
                    take(e, "down")

            act.wait_ge(ld_small, 16 * n_small)
            for h in range(HALVES):
                high_part(h)
                if h == 2 * STAGES - 1:
                    take_x1(0, 0, 0)
            take_x1(0, 0, 1)
            take_x1(0, 0, 2)
            act.wait_ge(early_done, 1)
            act.wait_ge(w_l, HALVES)
            tanh_of_gap(0, GT)
            gelu(0, 0, GT)
            with act.Fori(0, (NG - 2) // 2) as i:
                for par in range(2):
                    experts(i * 2 + par, par, GT, GT)
            experts(NG - 2, 0, GT, GT)
            experts(NG - 1, 1, GT, 1)
            experts(NG, 0, 1, 0)

        @block.vector
        def _(dve):
            seq = dve.alloc_register("dve_steps")
            dve.reg_mov(seq, 0)

            def chain(*steps):
                for step in steps:
                    step().then_inc(dve_seq, 1)
                    dve.reg_add(seq, seq, 1)
                    dve.wait_ge(dve_seq, dve.snap(seq, min_val=0, max_val=1 << 20))
                    dve.sem_inc(dve_go, 1)

            def rsqrt_steps(rows, n):
                v, r, t = ve[0:rows, 0:n], rs[0:rows, 0:n], rt[0:rows, 0:n]
                steps = [
                    lambda: dve.tensor_scalar(r.bitcast(I32), v.bitcast(I32), 1, None, ALU.logical_shift_right),
                    lambda: dve.tensor_scalar(r.bitcast(I32), r.bitcast(I32), -1.0, float(0x5F3759DF), ALU.mult, ALU.add),
                ]
                for _ in range(3):
                    steps += [
                        lambda: dve.tensor_tensor(t, r, r, ALU.mult),
                        lambda: dve.scalar_tensor_tensor(out=t, in0=t, scalar=-0.5, in1=v, op0=ALU.mult, op1=ALU.mult),
                        lambda: dve.scalar_tensor_tensor(out=r, in0=t, scalar=1.5, in1=r, op0=ALU.add, op1=ALU.mult),
                    ]
                return steps

            def each(tiles, f):
                def step():
                    for k in range(tiles):
                        last = f(k)
                    return last
                return step

            def statistics(rows, tiles, source, stat, a=1.0, b=EPS):
                chain(
                    each(tiles, lambda k: dve.bn_stats(stat[0:rows, k, :], source(k))),
                    each(tiles, lambda k: dve.bn_aggr(mv[0:rows, k, :], stat[0:rows, k, :])),
                    lambda: dve.tensor_scalar(ve[0:rows, 0:tiles], mv[0:rows, 0:tiles, 1], a, b, ALU.mult,
                                              ALU.add),
                    *rsqrt_steps(rows, tiles),
                )

            def centre(rows, k, source, target):
                return dve.tensor_scalar(target, source, mv[0:rows, k, 0:1], rs[0:rows, k:k + 1],
                                         ALU.subtract, ALU.mult)

            dve.sem_inc(y2_add, GT)
            dve.memset(wraw[:, :, :, :], 0.0).then_inc(fill, 1)
            dve.memset(e_src[:, EB - 1, :], 0)
            dve.memset(e_rel[:, EB - 1, :], 0)
            dve.memset(e_dst[:, EB - 1, :], N - 1)
            dve.memset(xall[:, FULL, :], 0.0)
            dve.memset(e_norm[:, EB - 1, :], 0.0).then_inc(fill, 1)
            dve.memset(ones[:, :], 1.0)
            dve.memset(zero_r[:, :].bitcast(F32), 0.0)
            dve.memset(span_lo[:, :], 0)
            dve.memset(span_n[:, :], NEVER)

            dve.wait_ge(ld_edge, 16 * 12)
            dve.tensor_copy(rowf[:, :, :], e_src[:, :, :])
            dve.tensor_copy(dstf[:, :, :], e_dst[:, :, :]).then_inc(edge_f, 1)
            dve.wait_ge(edge_f, 1)
            dve.tensor_reduce(mnmx[:, 0, :], dstf[:, :, :], AX.X, ALU.min)
            dve.tensor_reduce(mnmx[:, 1, :], dstf[:, :, :], AX.X, ALU.max).then_inc(edge_f, 1)
            dve.scalar_tensor_tensor(out=rowf[:, :, :], in0=rowf[:, :, :], scalar=float(R), in1=e_rel[:, :, :],
                                     op0=ALU.mult, op1=ALU.add).then_inc(edge_f, 1)
            dve.wait_ge(edge_f, 3)
            dve.wait_ge(pool_const, 5)
            for i in range(2 * EB):
                if i >= 2:
                    dve.wait_ge(pe_edge, 3 + i - 1)
                dve.tensor_scalar(diag[:, i % 2, :], ident[:, :], mnmx[:, i // EB, i % EB:i % EB + 1], None,
                                  ALU.mult).then_inc(diag_rdy, 1)

            def make_spans():
                dve.wait_ge(pe_edge, 3 + 2 * EB)
                dve.wait_ge(ld_small, 16 * n_small)
                chain(
                    lambda: dve.tensor_scalar(ends[:, 1:2], ends[:, 0:1], float(TN), None, ALU.add),
                    lambda: dve.tensor_scalar(hit[:, :], bank[7][0:NT, 0:EC], ends[:, 0:1], None, ALU.is_ge),
                    lambda: dve.scalar_tensor_tensor(out=hit[:, :], in0=bank[6][0:NT, 0:EC], scalar=ends[:, 1:2],
                                                     in1=hit[:, :], op0=ALU.is_lt, op1=ALU.mult),
                    lambda: dve.scalar_tensor_tensor(out=hit2[:, :], in0=iota_t[:, :], scalar=1.0, in1=hit[:, :],
                                                     op0=ALU.add, op1=ALU.mult),
                    lambda: dve.tensor_reduce(lohi[:, 1:2], hit2[:, :], AX.X, ALU.max),
                    lambda: dve.scalar_tensor_tensor(out=hit2[:, :], in0=hit[:, :], scalar=-FAR, in1=iota_t[:, :],
                                                     op0=ALU.mult, op1=ALU.add),
                    lambda: dve.tensor_reduce(lohi[:, 0:1], hit2[:, :], AX.X, ALU.min),
                    lambda: dve.tensor_scalar(lohi[:, 2:3], lohi[:, 0:1], FAR, float(EC - 1), ALU.add, ALU.min),
                    lambda: dve.scalar_tensor_tensor(out=lohi[:, 3:4], in0=lohi[:, 1:2], scalar=QC - 1.0, in1=lohi[:, 2:3],
                                                     op0=ALU.add, op1=ALU.subtract),
                    lambda: dve.tensor_scalar(lohi_i[:, 0:1], lohi[:, 3:4], least_s[:, 0:1], None, ALU.max),
                    lambda: dve.tensor_scalar(lohi_i[:, 1:2], lohi_i[:, 0:1], 2, None, ALU.arith_shift_right),
                )
                dve.tensor_copy(lohi[:, 3:4], lohi_i[:, 1:2]).then_inc(span_col, 1)
                dve.wait_ge(pe_edge, 4 + 2 * EB)
                dve.tensor_copy(span_lo[:, 0:NT], bank[6][0:1, 0:NT])
                chain(
                    lambda: dve.tensor_reduce(hit[0:1, 0:1], bank[6][0:1, 32:32 + NT], AX.X, ALU.add),
                    lambda: dve.tensor_scalar(turns_s[:, 0:1], hit[0:1, 0:1], RING - 1.0, None, ALU.add),
                    lambda: dve.tensor_scalar(turns_s[:, 1:2], turns_s[:, 0:1], RING.bit_length() - 1, None,
                                              ALU.arith_shift_right),
                )
                dve.tensor_copy(span_n[:, 0:NT], bank[6][0:1, 32:32 + NT]).then_inc(span_rdy, 1)
                dve.wait_ge(span_rdy, 1)
                dve.wait_ge(table_rdy, 1)

            def loaded_x(k):
                if k % (FULL // 4) == 0:
                    dve.wait_ge(ld_x[k // (FULL // 4)], 16)
                return xall[:, k, :]

            statistics(P, FULL + 1, loaded_x, stat_x)

            def normalise_x(t, par):
                if not (isinstance(t, int) and t < 2):
                    dve.wait_ge(xp_t, t - 1)
                at = bass.ds(t, 1)
                dve.tensor_scalar(xnorm[:, par, :], xall[:, at, :].rearrange("p a d -> p (a d)"),
                                  mv[:, at, 0], rs[:, at], ALU.subtract, ALU.mult).then_inc(xhat_rdy, 1)

            def low_part(t, par):
                dve.wait_ge(xp_h, t + 1)
                dve.tensor_tensor(xpl[:, par, :, :].rearrange("p c n -> p (c n)"), bank_tp[par][:, 0:D],
                                  xph[:, par, :, :].rearrange("p c n -> p (c n)"), ALU.subtract).then_inc(xp_l, 1)

            def copy_y(t, j, u):
                dve.wait_ge(y_mm, t * 4 + u + 1)
                dve.tensor_copy(ybuf[:, j, 4:8, u // 2, :],
                                bank_y[u][:, :].rearrange("p (r g) -> p r g", g=P)).then_inc(y_ev_v, 1)

            def tile_y(i, j):
                t = i * YB + j
                if not (isinstance(t, int) and t + 2 > FULL):
                    normalise_x(t + 2, j % 2)
                if not (isinstance(t, int) and t + 1 > FULL):
                    low_part(t + 1, (j + 1) % 2)
                if not (isinstance(i, int) and i == 0):
                    dve.wait_ge(y_st[j], i * 16)
                copy_y(t, j, 1)
                copy_y(t, j, 3)

            normalise_x(0, 0)
            normalise_x(1, 1)
            low_part(0, 0)
            for j in range(YB):
                tile_y(0, j)
            with dve.Fori(1, FULL // YB - 1) as i:
                for j in range(YB):
                    tile_y(i, j)
            for t in range(FULL - YB, FULL + 1):
                tile_y(t // YB, t % YB)
            make_spans()

            y_stored(dve)
            for t in (xth, xtl):
                gaps = t[:, :, :, :].rearrange("p a c (k s) -> p (a c k) s", s=SLOT)[:, :, TN:SLOT]
                last = dve.memset(gaps.bitcast(F32), 0.0)
            last.then_inc(early_done, 1)

            def low_part_of_half(h):
                _, stage, high, low = half(h)
                dve.wait_ge(w_h, h + 1)
                dve.tensor_tensor(low, stage, high, ALU.subtract).then_inc(w_l, 1)

            batch = dve.alloc_register("dve_batch")
            ecol = dve.alloc_register("dve_col")
            left = dve.alloc_register("dve_left")
            dve.reg_mov(batch, 0)

            def match_batch(m_set, again):
                b = dve.snap(batch, min_val=0, max_val=NEVER * NT)
                c = dve.snap(ecol, min_val=0, max_val=ECP - QC)
                if not again:
                    dve.wait_ge(m_used, b * QC + 1)
                for j in range(QC):
                    if again:
                        dve.wait_ge(m_used, b * QC + (j + 2))
                    dve.tensor_scalar(m_s[:, m_set * QC + j, :], iota_s[:, :], dst_t[:, bass.ds(c + j, 1)],
                                      norm_t[:, bass.ds(c + j, 1)], ALU.is_equal, ALU.mult).then_inc(m_rdy, 1)
                dve.reg_add(batch, batch, 1)
                dve.reg_add(ecol, ecol, QC)

            def match_first(g, k, part, m_set):
                if part == 0:
                    dve.reg_load(ecol, span_lo[0:1, bass.ds(g * GT + k, 1)])
                    if not (isinstance(g, int) and g * GT + k == 0):
                        dve.wait_ge(m_rdy, dve.snap(batch, min_val=1, max_val=NEVER * NT) * QC)
                    dve.tensor_scalar(iota_s[:, :], iota[:, :], starts[:, bass.ds(g * GT + k, 1)], None,
                                      ALU.add).then_inc(iota_rdy, 1)
                    dve.wait_ge(iota_rdy, g * GT + k + 1)
                    dve.sem_inc(dve_go, 1)
                match_batch(m_set, False)

            def match_rest(g, k, part, parts, m_set):
                dve.reg_mov(left, part_of(dve, g, k, part, parts))
                with dve.If_ne(left, 1):
                    with dve.Fori(1, dve.snap(left, min_val=2, max_val=NEVER)):
                        match_batch(m_set, True)
                    dve.sem_inc(dve_go, 1)

            def both_statistics(g, par, tiles):
                dve.wait_ge(x1_rdy, g * GT + tiles)
                statistics(TN, tiles, lambda k: x1[0:TN, par, k, :], stat, 1.0 + EPS, EPS * EPS)

            def normalise(g, par, tiles):
                each(tiles, lambda k: centre(TN, k, x1[0:TN, par, k, :], xz[0:TN, k, :]))().then_inc(z_rdy, 1)

            def activations(g, par, first, tiles):
                last_k = min(first + 2, tiles)
                dve.wait_ge(t_made, g * 4 + first // 2 + 1)
                for k in range(first, last_k):
                    for c in range(DC):
                        at = (k - first) * D + c * P
                        last = dve.tensor_scalar(xtf[:, c, k * SLOT:k * SLOT + TN], bank_t[:, at:at + TN],
                                                 gam[:, c:c + 1], bet[:, c:c + 1], ALU.mult, ALU.add)
                last.then_inc(t_read, 1)
                dve.wait_ge(t_read, g * 4 + first // 2 + 1)
                for k in range(first, last_k):
                    f = slice(k * SLOT, k * SLOT + TN)
                    last = dve.tensor_copy(xth[:, par, :, f], xtf[:, :, f])
                chain(lambda: last)
                for k in range(first, last_k):
                    f = slice(k * SLOT, k * SLOT + TN)
                    dve.tensor_tensor(xtl[:, par, :, f], xtf[:, :, f], xth[:, par, :, f], ALU.subtract).then_inc(xt_rdy, 1)

            def rank(g, tiles):
                use = (tiles + 1) // 2
                dve.wait_ge(t_made, g * 4 + use + 1)
                for k in range(tiles):
                    last = dve.tensor_tensor(logit[0:TN, k, :], bank_t[0:TN, k * X:(k + 1) * X], br_s[0:TN, :], ALU.add)
                last.then_inc(t_read, 1)
                dve.wait_ge(t_read, g * 4 + use + 1)
                dve.sem_inc(dve_go, 1)
                chain(
                    each(tiles, lambda k: dve.max(mx8[0:TN, k, :], logit[0:TN, k, :])),
                    each(tiles, lambda k: dve.max_index(ix8[0:TN, k, :], mx8[0:TN, k, :], logit[0:TN, k, :])),
                )
                dve.tensor_tensor(dlt[0:TN, 0:tiles], mx8[0:TN, 0:tiles, 0], mx8[0:TN, 0:tiles, 1],
                                  ALU.subtract).then_inc(dlt_rdy, 1)
                dve.tensor_copy(ixf[0:TN, 0:tiles, :], ix8[0:TN, 0:tiles, :])

            def weigh(g, tiles):
                dve.wait_ge(tnh_rdy, g + 1)
                if not (isinstance(g, int) and g == 0):
                    dve.wait_ge(y2_add, g * (GT * X) + GT)
                chain(
                    lambda: (dve.tensor_scalar(w12[0:TN, 0, 0:tiles], tnh[0:TN, 0:tiles], 0.5, 0.5, ALU.mult, ALU.add),
                             dve.tensor_scalar(w12[0:TN, 1, 0:tiles], tnh[0:TN, 0:tiles], -0.5, 0.5, ALU.mult, ALU.add))[1],
                    lambda: (each(tiles, lambda k: dve.tensor_scalar(
                        wfull[0:TN, k, :], iota8[0:TN, :], ixf[0:TN, k, 0:1], w12[0:TN, 0, k:k + 1],
                        ALU.is_equal, ALU.mult))(),
                        each(tiles, lambda k: dve.tensor_scalar(
                            logit[0:TN, k, :], iota8[0:TN, :], ixf[0:TN, k, 1:2], w12[0:TN, 1, k:k + 1],
                            ALU.is_equal, ALU.mult))())[1],
                )
                dve.tensor_tensor(wfull[0:TN, 0:tiles, :], wfull[0:TN, 0:tiles, :], logit[0:TN, 0:tiles, :],
                                  ALU.add).then_inc(wf_rdy, 1)

            def take_weights(g, tiles):
                use = (tiles + 1) // 2 + 1
                dve.wait_ge(t_made, g * 4 + use + 1)
                for k in range(tiles):
                    last = dve.tensor_copy(wft[:, k * SLOT:k * SLOT + TN], bank_t[0:X, k * SLOT:k * SLOT + TN])
                last.then_inc(wft_rdy, 1)
                dve.wait_ge(wft_rdy, g + 1)
                dve.sem_inc(t_read, 1)

            def add_bias2(g, par, tiles):
                for k in range(tiles):
                    dve.wait_ge(b_mm, g * GT + k + 1)
                    dve.wait_ge(y2_add, g * (GT * X) + GT + k + 1)
                    dve.tensor_tensor(x1[0:TN, par, k, :], bank_o[k][0:TN, 0:D], x1[0:TN, par, k, :],
                                      ALU.add).then_inc(b_add, 1)

            def low_parts(g, e, tiles):
                cols = tiles * SLOT
                for hc in range(HC):
                    dve.wait_ge(h_act, g * (X * HC) + e * HC + hc + 1)
                    dve.tensor_tensor(hl[:, e % 2, hc, 0:cols], hidden[:, e % 2, hc, 0:cols],
                                      hh[:, e % 2, hc, 0:cols], ALU.subtract).then_inc(h_split, 1)

            def add(g, par, e, tiles):
                for k in range(tiles):
                    dve.wait_ge(y2_mm, g * (GT * X) + e * tiles + k + 1 + GT)
                    if e == 1:
                        dve.wait_ge(b_add, g * GT + k + 1)
                    elif e:
                        dve.wait_ge(y2_add, GT + g * (GT * X) + (e - 1) * tiles + k + 1)
                    dve.scalar_tensor_tensor(out=x1[0:TN, par, k, :], in0=bank_o[k][0:TN, 0:D],
                                             scalar=wfull[0:TN, k, e:e + 1], in1=x1[0:TN, par, k, :],
                                             op0=ALU.mult, op1=ALU.add).then_inc(y2_add, 1)

            places = [at for at in PARTS]

            def begin_part(g, i, tiles):
                if i < len(places) and PARTS[places[i]][0] < tiles:
                    match_first(g, *PARTS[places[i]], i % 2)

            def experts(g, par, tiles, ahead, ahead2):
                def match(e, place):
                    k, part = PARTS.get((e, place), (GT, 0))
                    if k < ahead:
                        i = places.index((e, place))
                        match_rest(g + 1, k, part, PIECES[k], i % 2)
                        begin_part(g + 1, i + 1, ahead)

                for e in range(X):
                    match(e, "up")
                    if e == 1:
                        add_bias2(g, par, tiles)
                    if e == X - 2 and ahead:
                        activations(g + 1, 1 - par, 0, ahead)
                    if e == X - 1 and ahead:
                        rank(g + 1, ahead)
                    if e + 1 < X:
                        low_parts(g, e + 1, tiles)
                    elif ahead:
                        low_parts(g + 1, 0, ahead)
                    match(e, "down")
                    if e == 0:
                        take_weights(g, tiles)
                    if e == X - 4 and ahead:
                        both_statistics(g + 1, 1 - par, ahead)
                    if e == X - 3 and ahead:
                        normalise(g + 1, 1 - par, ahead)
                    if e == X - 2 and ahead > 2:
                        activations(g + 1, 1 - par, 2, ahead)
                    if e == X - 1 and ahead2:
                        begin_part(g + 2, 0, ahead2)
                    add(g, par, e, tiles)
                if ahead:
                    weigh(g + 1, ahead)

            splits = ((0, 2 * STAGES), (2 * STAGES, HALVES), (HALVES, HALVES))
            for k in range(GT):
                match_first(0, k, 0, (GT - k) % 2)
                for h in range(*splits[k]):
                    low_part_of_half(h)
                match_rest(0, k, 0, 1, (GT - k) % 2)
            both_statistics(0, 0, GT)
            normalise(0, 0, GT)
            activations(0, 0, 0, GT)
            activations(0, 0, 2, GT)
            rank(0, GT)
            low_parts(0, 0, GT)
            begin_part(1, 0, GT)
            weigh(0, GT)
            with dve.Fori(0, (NG - 2) // 2) as i:
                for par in range(2):
                    experts(i * 2 + par, par, GT, GT, GT)
            experts(NG - 2, 0, GT, GT, 1)
            experts(NG - 1, 1, GT, 1, 0)
            experts(NG, 0, 1, 0, 0)


def kernel(x, src, dst, edge_type_8, edge_weight, L0_gnn_weight, L0_ffn_gamma, L0_ffn_beta, L0_ffn_Wr, L0_ffn_br,
           L0_ffn_W1, L0_ffn_b1, L0_ffn_W2, L0_ffn_b2):
    from concourse import bacc
    from concourse.bass_utils import run_bass_kernel_spmd

    first_nodes = TN * np.array(ORDER)
    ins = {
        "x": x, "src": src, "dst": dst, "rel": edge_type_8, "norm": edge_weight,
        "gnn_w": np.asarray(L0_gnn_weight).reshape(R, NB * SB * SB), "gamma": L0_ffn_gamma, "beta": L0_ffn_beta,
        "wr": L0_ffn_Wr, "br": L0_ffn_br, "w1": L0_ffn_W1, "b1": L0_ffn_b1, "w2": L0_ffn_W2, "b2": L0_ffn_b2,
        "starts_f": first_nodes.astype(np.float32), "starts_i": first_nodes.astype(np.int32).reshape(1, NT),
        "least": QC * np.array([LEAST[i % GT] for i in range(NT)], np.float32),
    }
    ins = {name: np.ascontiguousarray(a) for name, a in ins.items()}
    nc = bacc.Bacc("TRN2", target_bir_lowering=False, num_devices=1)
    aps = {name: nc.dram_tensor(f"in_{name}", a.shape, mybir.dt.from_np(a.dtype), kind="ExternalInput").ap()
           for name, a in ins.items()}
    out = nc.dram_tensor("out_x", (N, D), F32, kind="ExternalOutput").ap()
    build_program(nc, out=out, **aps)
    r = run_bass_kernel_spmd(nc, [{f"in_{name}": a for name, a in ins.items()}], core_ids=[0])
    return r.results[0]["out_x"]
```

```python
from contextlib import ExitStack

import numpy as np

import concourse.bass as bass
from concourse import mybir

F32 = mybir.dt.float32
F32R = mybir.dt.float32r
I32 = mybir.dt.int32
U32 = mybir.dt.uint32
ALU = mybir.AluOpType
ACT = mybir.ActivationFunctionType
AX = mybir.AxisListType

P = 128
N, D = 3125, 256
E = 50000
R = 8
NB = 8
SB = D // NB
X, H = 8, 512
DC, HC = D // P, H // P
EPS = 1e-5

TN = 125
NT = N // TN
GT = 3
NG = NT // GT
PAD = GT - 1
SLOT = TN
COLS = GT * SLOT + GT * SLOT % 2
FULL = N // P
REST = N - FULL * P
YB = 4
HALVES = 2 * X
STAGES = 6
EC = (E + P - 1) // P
EB = (EC + P - 1) // P
QC = 4
SHORTEST = 2
LEAST = (4, 2, 2)
ECP = EC + QC * max(LEAST)
RING = 4
LAG = 1
NEVER = 4096
FAR = 1.0e4

ORDER = [24, 7, 23, 22, 0, 21, 20, 1, 19, 18, 2, 17, 16, 3, 15, 14, 4, 13, 12, 5, 11, 10, 6, 9, 8]
PIECES = (4, 2, 2)
PARTS = {(0, "up"): (0, 0), (1, "up"): (0, 1), (2, "up"): (0, 2), (3, "up"): (0, 3),
         (3, "down"): (1, 0), (4, "up"): (1, 1), (4, "down"): (2, 0), (5, "up"): (2, 1)}
assert all(a <= b for a, b in zip(PIECES, LEAST)) and ECP <= EB * P and len(PARTS) % 2 == 0
assert NT * TN == N and NG * GT + 1 == NT and sorted(ORDER) == list(range(NT))


def build_program(nc, x, src, dst, rel, norm, gnn_w, gamma, beta, wr, br, w1, b1, w2, b2,
                  starts_f, starts_i, least, out):
    y = nc.dram_tensor("y_rows", [N * R, D], F32).ap()
    y_nodes = y.rearrange("(n r) d -> n (r d)", r=R)

    top = ExitStack()
    with top:
        def sb(stack, name, shape, dt=F32):
            return stack.enter_context(nc.sbuf_tensor(name, shape, dt))

        def sem(name):
            return top.enter_context(nc.semaphore(name))

        bank = [top.enter_context(nc.psum_tensor(f"bank{i}", [P, 512], F32)) for i in range(8)]

        row_t = sb(top, "row_t", [P, ECP], I32)
        dst_t = sb(top, "dst_t", [P, ECP])
        norm_t = sb(top, "norm_t", [P, ECP])
        ident = sb(top, "ident", [P, P])
        iota = sb(top, "iota", [P, TN])
        starts = sb(top, "starts", [P, NT])
        starts_r = sb(top, "starts_r", [1, 32], I32)
        span_lo = sb(top, "span_lo", [1, 32], I32)
        span_n = sb(top, "span_n", [1, 32], I32)
        turns_s = sb(top, "turns_s", [1, 2], I32)
        gam = sb(top, "gam", [P, DC])
        bet = sb(top, "bet", [P, DC])
        wr_s = sb(top, "wr_s", [P, DC, X])
        br_s = sb(top, "br_s", [P, X])
        b1_s = sb(top, "b1_s", [P, X, HC])
        b2_s = sb(top, "b2_s", [X, D])
        iota8 = sb(top, "iota8", [P, X])
        zero_r = sb(top, "zero_r", [P, TN + 1], F32R)
        mv = sb(top, "mv", [P, FULL + 1, 2])
        rs = sb(top, "rs", [P, FULL + 1])
        rt = sb(top, "rt", [P, FULL + 1])
        ve = sb(top, "ve", [P, FULL + 1])

        with ExitStack() as staging:
            w_stage = sb(staging, "w_stage", [P, STAGES, DC * H])
        hh = sb(top, "hh", [P, 2, HC, COLS], F32R)
        with ExitStack() as staging:
            hidden = sb(staging, "hidden", [P, 2, HC, COLS])
        hl = sb(top, "hl", [P, 2, HC, COLS], F32R)
        xtf = sb(top, "xtf", [P, DC, COLS])

        with ExitStack() as early:
            xall = sb(early, "xall", [P, FULL + 1, D])
            stat_x = sb(early, "stat_x", [P, FULL + 1, 6])
            xnorm = sb(early, "xnorm", [P, 2, D])
            wbh = sb(early, "wbh", [P, DC, R, P], F32R)
            wbl = sb(early, "wbl", [P, DC, R, P], F32R)
            xph = sb(early, "xph", [P, 2, DC, P], F32R)
            xpl = sb(early, "xpl", [P, 2, DC, P], F32R)
            ybuf = sb(early, "ybuf", [P, YB, R, DC, P])
            wraw = sb(early, "wraw", [P, DC, R, P])
            e_src = sb(early, "e_src", [P, EB, P], I32)
            e_dst = sb(early, "e_dst", [P, EB, P], I32)
            e_rel = sb(early, "e_rel", [P, EB, P], I32)
            e_norm = sb(early, "e_norm", [P, EB, P])
            rowf = sb(early, "rowf", [P, EB, P])
            dstf = sb(early, "dstf", [P, EB, P])
            diag = sb(early, "diag", [P, 2 * EB, P])
            iota_t = sb(early, "iota_t", [NT, EC])
            hit = sb(early, "hit", [NT, EC])
            hit2 = sb(early, "hit2", [NT, EC])
            ones = sb(early, "ones", [P, NT])
            mnmx = sb(early, "mnmx", [P, 2, EB])
            ends = sb(early, "ends", [NT, 2])
            least_s = sb(early, "least_s", [NT, 1])
            lohi = sb(early, "lohi", [NT, 4])
            lohi_i = sb(early, "lohi_i", [NT, 2], I32)

        w1h = sb(top, "w1h", [P, DC, X, H], F32R)
        w1l = sb(top, "w1l", [P, DC, X, H], F32R)
        w2h = sb(top, "w2h", [P, HC, X, D], F32R)
        w2l = sb(top, "w2l", [P, HC, X, D], F32R)
        gath = sb(top, "gath", [P, QC * RING, D])
        idx = sb(top, "idx", [P, QC * RING], I32)
        m_s = sb(top, "m_s", [P, 3 * QC, TN])
        iota_s = sb(top, "iota_s", [P, TN])
        xth = sb(top, "xth", [P, 2, DC, COLS], F32R)
        xtl = sb(top, "xtl", [P, 2, DC, COLS], F32R)
        xz = sb(top, "xz", [P, GT, D])
        x1 = sb(top, "x1", [P, 2, GT, D])
        stat = sb(top, "stat", [P, GT, 6])
        logit = sb(top, "logit", [P, GT, X])
        mx8 = sb(top, "mx8", [P, GT, X])
        ix8 = sb(top, "ix8", [P, GT, X], U32)
        ixf = sb(top, "ixf", [P, GT, X])
        dlt = sb(top, "dlt", [P, GT])
        tnh = sb(top, "tnh", [P, GT])
        w12 = sb(top, "w12", [P, 2, GT])
        wfull = sb(top, "wfull", [P, GT, X])
        wft = xtf[0:X, :, :].rearrange("p c n -> p (c n)")

        ld_edge = sem("ld_edge")
        ld_x = [sem(f"ld_x{i}") for i in range(5)]
        ld_wb = sem("ld_wb")
        ld_small = sem("ld_small")
        ld_w = [sem(f"ld_w{i}") for i in range(STAGES)]
        pool_const = sem("pool_const")
        fill = sem("fill")
        edge_f = sem("edge_f")
        diag_rdy = sem("diag_rdy")
        pe_edge = sem("pe_edge")
        span_col = sem("span_col")
        span_rdy = sem("span_rdy")
        dve_seq = sem("dve_seq")
        dve_go = sem("dve_go")
        pool_go = sem("pool_go")
        xhat_rdy = sem("xhat_rdy")
        wb_h = sem("wb_h")
        wb_l = sem("wb_l")
        xp_t = sem("xp_t")
        xp_h = sem("xp_h")
        xp_l = sem("xp_l")
        y_mm = sem("y_mm")
        y_ev_a = sem("y_ev_a")
        y_ev_v = sem("y_ev_v")
        y_st = [sem(f"y_st{i}") for i in range(YB)]
        w_h = sem("w_h")
        w_l = sem("w_l")
        table_rdy = sem("table_rdy")
        early_done = sem("early_done")
        idx_rdy = sem("idx_rdy")
        land = [sem(f"land{i}") for i in range(RING)]
        landed = sem("landed")
        m_used = sem("m_used")
        m_rdy = sem("m_rdy")
        iota_rdy = sem("iota_rdy")
        ld_xin = [sem(f"ld_xin{i}") for i in range(GT)]
        x1_rdy = sem("x1_rdy")
        z_rdy = sem("z_rdy")
        t_made = sem("t_made")
        t_read = sem("t_read")
        xt_rdy = sem("xt_rdy")
        wf_rdy = sem("wf_rdy")
        wft_rdy = sem("wft_rdy")
        dlt_rdy = sem("dlt_rdy")
        tnh_rdy = sem("tnh_rdy")
        b_mm = sem("b_mm")
        b_add = sem("b_add")
        h_mm = sem("h_mm")
        h_act = sem("h_act")
        h_split = sem("h_split")
        y2_mm = sem("y2_mm")
        y2_add = sem("y2_add")
        st_out = [sem(f"st_out{i}") for i in range(GT)]

        bank_y, bank_tp = bank[0:4], bank[4:6]
        bank_h, bank_o, bank_acc, bank_t = bank[0:3], bank[3:6], bank[6], bank[7]

        gnn_v = gnn_w.rearrange("r (b i o) -> b i r o", b=NB, i=SB)
        w1_v = w1.rearrange("e (c p) h -> e p c h", p=P)
        w2_v = w2.rearrange("e (c p) d -> e p c d", p=P)
        n_small = 10
        full_rows = E // P
        rest_e = E - full_rows * P
        eb_full = full_rows // P
        eb_rest = full_rows - eb_full * P

        def place_of(g, k):
            return 0 if isinstance(g, int) and g == 0 else g * GT + (k - PAD)

        def count(g, k):
            return PAD if isinstance(g, int) and g == 0 else g * GT + k

        def use_of(g, i):
            return i + 1 if isinstance(g, int) and g == 0 else g * 4 + i

        def outputs(g, e, k, tiles):
            return (PAD * X if isinstance(g, int) and g == 0 else g * (GT * X)) + (e * tiles + k)

        def part_of(engine, g, k, part, parts):
            n = engine.value_load(span_n[0:1, bass.ds(place_of(g, k), 1)],
                                  min_val=SHORTEST if parts == 1 else min(LEAST), max_val=NEVER)
            return n if parts == 1 else (n + part) // parts

        block = top.enter_context(nc.Block())

        def hidden_bank(e, hc, tiles):
            if tiles == GT or e == 0:
                return bank_h[(e + hc) % 3], 2 if e == 0 and hc < 2 else 3
            five = [*bank_h, *bank_o[1:3]]
            return five[(e * HC + hc) % 5], 2 if e == 1 else 5

        def y_stored(engine):
            for i in range(YB):
                engine.wait_ge(y_st[i], 16 * (FULL // YB) + (32 if i == FULL % YB else 0))

        def half(h):
            e, stage = h // 2, w_stage[:, h % STAGES, :]
            if h % 2 == 0:
                return w1_v[e], stage.rearrange("p (c h) -> p c h", c=DC), w1h[:, :, e, :], w1l[:, :, e, :]
            return w2_v[e], stage.rearrange("p (c d) -> p c d", c=HC), w2h[:, :, e, :], w2l[:, :, e, :]

        @block.sync
        def _(sp):
            for k in range(GT):
                sp.sem_inc(st_out[k], 32 if k else 16)
                if k:
                    sp.sem_inc(ld_xin[k], 16)
            q = FULL // 4
            for c in range(4):
                sp.dma_start(xall[:, c * q:(c + 1) * q, :],
                             x[c * q * P:(c + 1) * q * P, :].rearrange("(t p) d -> p t d", p=P)).then_inc(ld_x[c], 16)
            arrays = ((src, e_src), (dst, e_dst), (rel, e_rel), (norm, e_norm))
            rows = [a[0:full_rows * P].rearrange("(t p) -> t p", p=P) for a, _ in arrays]
            for r, (a, t) in zip(rows, arrays):
                sp.dma_start(t[:, 0:eb_full, :],
                             r[0:eb_full * P].rearrange("(b t) p -> t b p", t=P)).then_inc(ld_edge, 16)
            sp.wait_ge(fill, 2)
            sp.dma_start(xall[0:REST, FULL, :], x[FULL * P:N, :]).then_inc(ld_x[4], 16)
            for r, (a, t) in zip(rows, arrays):
                sp.dma_start(t[0:eb_rest, eb_full, :], r[eb_full * P:full_rows]).then_inc(ld_edge, 16)
                sp.dma_start(t[eb_rest:eb_rest + 1, eb_full, 0:rest_e],
                             a[full_rows * P:E].rearrange("(a n) -> a n", a=1)).then_inc(ld_edge, 16)

            def store_y(t, j):
                sp.wait_ge(y_ev_a, t * 2 + 2)
                sp.wait_ge(y_ev_v, t * 2 + 2)
                sp.dma_start(y_nodes[bass.ds(t * P, P), :],
                             ybuf[:, j, :, :, :].rearrange("p r c g -> p (r c g)")).then_inc(y_st[j], 16)

            def load_half(h):
                there, stage, _, _ = half(h)
                sp.dma_start(stage, there).then_inc(ld_w[h % STAGES], 16)

            for h in range(STAGES):
                load_half(h)
            for t in range(YB):
                store_y(t, t)
            with sp.Fori(1, FULL // YB) as i:
                for j in range(YB):
                    store_y(i * YB + j, j)
            sp.wait_ge(y_ev_a, FULL * 2 + 2)
            sp.wait_ge(y_ev_v, FULL * 2 + 2)
            yb = ybuf[:, FULL % YB, :, :, :].rearrange("p r c g -> p (r c g)")
            k = REST // 16 * 16
            sp.dma_start(y_nodes[FULL * P:FULL * P + k, :], yb[0:k, :]).then_inc(y_st[FULL % YB], 16)
            sp.dma_start(y_nodes[FULL * P + k:N, :], yb[k:REST, :]).then_inc(y_st[FULL % YB], 16)

            def load_xin(g, k):
                start = sp.value_load(starts_r[0:1, bass.ds(place_of(g, k), 1)], min_val=0, max_val=N - TN)
                sp.dma_start(xz[0:TN, k, :], x[bass.ds(start, TN), :]).then_inc(ld_xin[k], 16)

            y_stored(sp)
            sp.wait_ge(ld_small, 16 * n_small)
            load_xin(0, 0)
            for h in range(STAGES, HALVES):
                sp.wait_ge(w_l, h - STAGES + 1)
                load_half(h)

            def store_out(g, par, tiles):
                for k in range(tiles):
                    sp.wait_ge(y2_add, outputs(g, X - 1, k, tiles) + (GT + 1))
                    start = sp.value_load(starts_r[0:1, bass.ds(place_of(g, k), 1)], min_val=0, max_val=N - TN)
                    sp.dma_start(out[bass.ds(start, TN), :], x1[0:TN, par, k, :]).then_inc(st_out[k], 16)

            def load_group(g):
                sp.wait_ge(t_made, g * 4 - 2)
                for k in range(GT):
                    load_xin(g, k)

            load_group(1)
            load_group(2)
            store_out(0, 0, 1)
            with sp.Fori(0, (NG - 2) // 2) as i:
                for j in range(2):
                    load_group(i * 2 + j + 3)
                    store_out(i * 2 + j + 1, (j + 1) % 2, GT)
            for g in range(NG - 1, NG + 1):
                store_out(g, g % 2, GT)
            for k in range(GT):
                sp.wait_ge(st_out[k], 16 * (NG + 2))

        @block.gpsimd
        def _(pool):
            pool.memset(ident[:, :], 0.0).then_inc(pool_const, 1)
            pool.wait_ge(pool_const, 1)
            pool.affine_select(out=ident[:, :], in_=ident[:, :], compare_op=ALU.not_equal, fill=1.0,
                               base=0, pattern=[[-1, P]], channel_multiplier=1).then_inc(pool_const, 1)
            pool.iota(iota[:, :], pattern=[[1, TN]], base=0, channel_multiplier=0,
                      allow_small_or_imprecise_dtypes=True).then_inc(pool_const, 1)
            pool.iota(iota8[:, :], pattern=[[1, X]], base=0, channel_multiplier=0,
                      allow_small_or_imprecise_dtypes=True).then_inc(pool_const, 1)
            pool.iota(iota_t[:, :], pattern=[[1, EC]], base=0, channel_multiplier=0,
                      allow_small_or_imprecise_dtypes=True).then_inc(pool_const, 1)
            pool.wait_ge(wb_h, 1)
            pool.tensor_tensor(wbl[:, :, :, :], wraw[:, :, :, :], wbh[:, :, :, :], ALU.subtract).then_inc(wb_l, 1)
            pool.wait_ge(table_rdy, 1)
            pool.wait_ge(span_rdy, 1)
            turns = pool.value_load(turns_s[0:1, 1:2], min_val=NT * SHORTEST // RING, max_val=NEVER * NT)
            col = pool.alloc_register("col")
            left = pool.alloc_register("left")
            at = pool.alloc_register("at")
            pool.reg_mov(at, 0)
            pool.reg_load(col, span_lo[0:1, 0:1])
            pool.reg_load(left, span_n[0:1, 0:1])
            y_stored(pool)

            def gather_batch(turn, j, first=False):
                if not (isinstance(turn, int) and turn == 0):
                    pool.wait_ge(m_used, (turn * RING + (j + 2 - RING)) * QC + 1)
                c = pool.snap(col, min_val=0, max_val=ECP - QC)
                own = slice(QC * j, QC * j + QC)
                pool.tensor_copy(idx[:, own], row_t[:, bass.ds(c, QC)]).then_inc(idx_rdy, 1)
                pool.reg_add(col, col, QC)
                pool.reg_sub(left, left, 1)
                with pool.If_eq(left, 0):
                    pool.reg_add(at, at, 1)
                    a = pool.snap(at, min_val=0, max_val=NT)
                    pool.reg_load(col, span_lo[0:1, bass.ds(a, 1)])
                    pool.reg_load(left, span_n[0:1, bass.ds(a, 1)])
                pool.wait_ge(idx_rdy, turn * RING + j + 1)
                pool.sem_inc(pool_go, 1)
                for s in range(QC * j, QC * j + QC):
                    if s == QC * j + QC // 2:
                        if not first:
                            pool.wait_ge(land[(j - LAG) % RING], (turn + (1 if j >= LAG else 0)) * (16 * QC))
                        pool.sem_inc(landed, 1)
                    pool.indirect_dma_start(
                        out=gath[:, s, :], out_offset=None, in_=y,
                        in_offset=bass.IndirectOffsetOnAxis(ap=idx[:, s:s + 1], axis=0),
                    ).then_inc(land[j], 16)

            for j in range(RING):
                gather_batch(0, j, j < LAG)
            with pool.Fori(1, turns) as turn:
                for j in range(RING):
                    gather_batch(turn, j)
            for j in range(LAG):
                pool.wait_ge(land[RING - LAG + j], turns * (16 * QC))
                pool.sem_inc(landed, 1)
            for j in range(RING):
                pool.wait_ge(land[j], turns * (16 * QC))

        @block.tensor
        def _(pe):
            def split_mm(outp, stat_h, stat_l, mov_h, mov_l, start, stop):
                pe.matmul(outp, stat_h, mov_h, start=start, stop=False)
                pe.matmul(outp, stat_h, mov_l, start=False, stop=False)
                return pe.matmul(outp, stat_l, mov_h, start=False, stop=stop)

            pe.sem_inc(y2_mm, GT + PAD * X)
            pe.sem_inc(b_mm, PAD)
            pe.sem_inc(t_made, 1)
            pe.sem_inc(m_used, QC + 1)
            def make_y(t, par):
                pe.wait_ge(xhat_rdy, t + 1)
                if not (isinstance(t, int) and t < 2):
                    pe.wait_ge(xp_l, t - 1)
                for c in range(DC):
                    last = pe.transpose(bank_tp[par][:, c * P:(c + 1) * P],
                                        xnorm[:, par, c * P:(c + 1) * P], ident[:, :])
                last.then_inc(xp_t, 1)

            def mul_y(t, par):
                pe.wait_ge(xp_l, t + 1)
                for u in range(4):
                    c, half = u // 2, u % 2
                    if not (isinstance(t, int) and t == 0):
                        pe.wait_ge(y_ev_v if half else y_ev_a, t * 2 + c - 1)
                    split_mm(bank_y[u][:, :], xph[:, par, c, :], xpl[:, par, c, :],
                             wbh[:, c, 4 * half:4 * half + 4, :].rearrange("p r g -> p (r g)"),
                             wbl[:, c, 4 * half:4 * half + 4, :].rearrange("p r g -> p (r g)"),
                             True, True).then_inc(y_mm, 1)

            def tile_y(t, j):
                if not (isinstance(t, int) and t == FULL):
                    make_y(t + 1, (j + 1) % 2)
                mul_y(t, j % 2)

            pe.wait_ge(pool_const, 2)
            make_y(0, 0)
            for i in range(2 * EB):
                pe.wait_ge(diag_rdy, i + 1)
                pe.matmul(bank[6 + i // EB][0:NT, (i % EB) * P:(i % EB + 1) * P], ones[:, :],
                          diag[:, i, :], start=True, stop=True).then_inc(pe_edge, 1)
            pe.wait_ge(wb_l, 1)
            for t in range(YB):
                tile_y(t, t)
            with pe.Fori(1, FULL // YB - 1) as i:
                for j in range(YB):
                    tile_y(i * YB + j, j)
            for t in range(FULL - YB, FULL + 1):
                tile_y(t, t % YB)
            pe.wait_ge(edge_f, 3)
            pe.wait_ge(y_ev_a, FULL * 2 + 2)
            pe.wait_ge(y_ev_v, FULL * 2 + 2)
            for b, t in enumerate((rowf, dstf, e_norm)):
                for k in range(EB):
                    last = pe.transpose(bank[b][:, k * P:(k + 1) * P], t[:, k, :], ident[:, :])
                last.then_inc(pe_edge, 1)
            pe.wait_ge(span_col, 1)
            for i in range(2):
                last = pe.transpose(bank[6][0:1, i * 32:i * 32 + NT], lohi[:, 2 + i:3 + i], ident[0:NT, 0:NT])
            last.then_inc(pe_edge, 1)

            batch = pe.alloc_register("pe_batch")
            slot = pe.alloc_register("pe_slot")
            pe.reg_mov(batch, 0)

            left = pe.alloc_register("pe_left")

            def sum_batch(m_set):
                b = pe.snap(batch, min_val=0, max_val=NEVER * NT)
                pe.reg_alu(slot, batch, RING - 1, ALU.bitwise_and)
                s = pe.snap(slot, min_val=0, max_val=RING - 1)
                pe.wait_ge(landed, b + 1 + LAG)
                for j in range(QC):
                    pe.wait_ge(m_rdy, b * QC + j + 1)
                    pe.matmul(bank_acc[0:TN, 0:D], m_s[:, m_set * QC + j, :],
                              gath[:, bass.ds(s * QC + j, 1), :].rearrange("p a d -> p (a d)"),
                              start=False, stop=False, skip_group_check=True).then_inc(m_used, 1)
                pe.reg_add(batch, batch, 1)

            def sum_part(g, k, part, parts, m_set):
                if part == 0:
                    if not (isinstance(g, int) and g == 0 and k == 0):
                        pe.wait_ge(x1_rdy, count(g, k))
                    pe.matmul(bank_acc[0:TN, 0:2], zero_r[:, 0:TN], zero_r[:, 0:2], start=True, stop=False,
                              skip_group_check=True)
                pe.reg_mov(left, part_of(pe, g, k, part, parts))
                sum_batch(m_set)
                with pe.If_ne(left, 1):
                    with pe.Fori(1, pe.snap(left, min_val=2, max_val=NEVER)):
                        sum_batch(2)

            def t_free(g, i):
                if not (isinstance(g, int) and g == 0 and i == 0):
                    pe.wait_ge(t_read, use_of(g, i))

            def turn_over(g, first, tiles):
                pe.wait_ge(z_rdy, g + 1)
                t_free(g, first // 2)
                for k in range(first, min(first + 2, tiles)):
                    for c in range(DC):
                        at = (k - first) * D + c * P
                        last = pe.transpose(bank_t[:, at:at + TN], xz[0:TN, k, c * P:(c + 1) * P], ident[0:TN, 0:TN])
                last.then_inc(t_made, 1)

            def route(g, tiles):
                use = (tiles + 1) // 2
                t_free(g, use)
                pe.wait_ge(xt_rdy, g * GT + GT)
                for k in range(tiles):
                    for c in range(DC):
                        last = pe.matmul(bank_t[0:TN, k * X:(k + 1) * X], xtf[:, c, k * SLOT:k * SLOT + TN],
                                         wr_s[:, c, :], start=(c == 0), stop=(c == DC - 1))
                last.then_inc(t_made, 1)

            def turn_weights(g, tiles):
                t_free(g, (tiles + 1) // 2 + 1)
                pe.wait_ge(wf_rdy, g + 1)
                for k in range(tiles):
                    last = pe.transpose(bank_t[0:X, k * SLOT:k * SLOT + TN], wfull[0:TN, k, :], ident[0:TN, 0:TN])
                last.then_inc(t_made, 1)

            def bias2(g, tiles):
                pe.wait_ge(wft_rdy, g + 1)
                for k in range(tiles):
                    pe.wait_ge(y2_add, outputs(g, 0, k, tiles) + (GT + 1))
                    pe.matmul(bank_o[k][0:TN, 0:D], wft[:, k * SLOT:k * SLOT + TN], b2_s[:, :],
                              start=True, stop=True).then_inc(b_mm, 1)

            def up(g, par, e, tiles):
                cols = tiles * SLOT + tiles * SLOT % 2
                if e == 0:
                    pe.wait_ge(xt_rdy, g * GT + GT)
                for hc in range(HC):
                    bank_of, back = hidden_bank(e, hc, tiles)
                    if not (isinstance(g, int) and g * X * HC + e * HC + hc < back):
                        pe.wait_ge(h_act, g * (X * HC) + (e * HC + hc + 1 - back))
                    for c in range(DC):
                        f = slice(hc * P, (hc + 1) * P)
                        last = split_mm(bank_of[:, 0:cols], w1h[:, c, e, f], w1l[:, c, e, f],
                                        xth[:, par, c, 0:cols], xtl[:, par, c, 0:cols], c == 0, c == DC - 1)
                    last.then_inc(h_mm, 1)

            def down(g, e, tiles):
                pe.wait_ge(h_split, g * (X * HC) + e * HC + HC)
                if e == 0 and not (isinstance(g, int) and g == 0):
                    pe.wait_ge(y2_add, g * (GT * X) + GT)
                for k in range(tiles):
                    if e == 1:
                        pe.wait_ge(b_add, count(g, k) + 1)
                    elif e:
                        pe.wait_ge(y2_add, outputs(g, e - 1, k, tiles) + (GT + 1))
                    for hc in range(HC):
                        f = slice(k * SLOT, k * SLOT + TN)
                        last = split_mm(bank_o[k][0:TN, 0:D], hh[:, e % 2, hc, f], hl[:, e % 2, hc, f],
                                        w2h[:, hc, e, :], w2l[:, hc, e, :], hc == 0, hc == HC - 1)
                    last.then_inc(y2_mm, 1)

            def experts(g, par, tiles, ahead):
                for e in range(X):
                    for place in ("up", "down"):
                        k, part = PARTS.get((e, place), (GT, 0))
                        if k < ahead:
                            sum_part(g + 1, k, part, PIECES[k], list(PARTS).index((e, place)) % 2)
                        if place == "up":
                            if e == 1:
                                bias2(g, tiles)
                            if e == X - 2 and ahead:
                                turn_over(g + 1, 0, ahead)
                            if e == X - 1 and ahead:
                                route(g + 1, ahead)
                            if e + 1 < X:
                                up(g, par, e + 1, tiles)
                            elif ahead:
                                up(g + 1, 1 - par, 0, ahead)
                        else:
                            if e == 0:
                                turn_weights(g, tiles)
                            if e == X - 2 and ahead > 2:
                                turn_over(g + 1, 2, ahead)
                            down(g, e, tiles)

            pe.wait_ge(span_rdy, 1)
            pe.wait_ge(early_done, 1)
            sum_part(0, 0, 0, 1, 1)
            turn_over(0, 0, 1)
            route(0, 1)
            pe.wait_ge(w_l, HALVES)
            up(0, 0, 0, 1)
            experts(0, 0, 1, GT)
            with pe.Fori(0, (NG - 2) // 2) as i:
                for j in range(2):
                    experts(i * 2 + j + 1, (j + 1) % 2, GT, GT)
            experts(NG - 1, 1, GT, GT)
            experts(NG, 0, GT, 0)

        @block.scalar
        def _(act):
            act.dma_start(starts_r[:, 0:NT], starts_i).then_inc(ld_small, 16)
            act.dma_start(starts[:, :], starts_f.partition_broadcast(P)).then_inc(ld_small, 16)
            act.wait_ge(fill, 1)
            for b in range(NB):
                c, q = b * SB // P, b * SB % P
                act.dma_start(wraw[q:q + SB, c, :, q:q + SB], gnn_v[b]).then_inc(ld_wb, 16)
            act.dma_start(ends[:, 0:1], starts_f.rearrange("(n a) -> n a", a=1)).then_inc(ld_small, 16)
            act.dma_start(least_s[:, :], least.rearrange("(n a) -> n a", a=1)).then_inc(ld_small, 16)
            with nc.allow_non_contiguous_dma(reason="small parameters, once"):
                act.dma_start(gam[:, :], gamma.rearrange("(c p) -> p c", p=P)).then_inc(ld_small, 16)
                act.dma_start(bet[:, :], beta.rearrange("(c p) -> p c", p=P)).then_inc(ld_small, 16)
                act.dma_start(b1_s[:, :, :].rearrange("p e c -> p (e c)"),
                              b1.rearrange("e (c p) -> p (e c)", p=P)).then_inc(ld_small, 16)
            act.dma_start(wr_s[:, :, :], wr.rearrange("(c p) e -> p c e", p=P)).then_inc(ld_small, 16)
            act.dma_start(br_s[:, :], br.partition_broadcast(P)).then_inc(ld_small, 16)
            act.dma_start(b2_s[:, :], b2).then_inc(ld_small, 16)
            act.wait_ge(ld_wb, 16 * NB)
            act.activation(wbh[:, :, :, :], wraw[:, :, :, :], ACT.Copy).then_inc(wb_h, 1)
            def part_of_y(t, par):
                act.wait_ge(xp_t, t + 1)
                act.activation(xph[:, par, :, :].rearrange("p c n -> p (c n)"), bank_tp[par][:, 0:D],
                               ACT.Copy).then_inc(xp_h, 1)

            def copy_y(t, j, u):
                act.wait_ge(y_mm, t * 4 + u + 1)
                act.activation(ybuf[:, j, 0:4, u // 2, :], bank_y[u][:, :].rearrange("p (r g) -> p r g", g=P),
                               ACT.Copy).then_inc(y_ev_a, 1)

            def tile_y(i, j):
                t = i * YB + j
                if not (isinstance(t, int) and t == FULL):
                    if not (isinstance(t, int) and t == 0):
                        act.wait_ge(y_mm, t * 4)
                    part_of_y(t + 1, (j + 1) % 2)
                if not (isinstance(t, int) and t < YB):
                    act.wait_ge(y_st[j], i * 16)
                copy_y(t, j, 0)
                copy_y(t, j, 2)

            part_of_y(0, 0)
            for t in range(YB):
                tile_y(0, t)
            with act.Fori(1, FULL // YB - 1) as i:
                for j in range(YB):
                    tile_y(i, j)
            for t in range(FULL - YB, FULL + 1):
                tile_y(t // YB, t % YB)

            act.wait_ge(pe_edge, 2 * EB + 3)
            act.activation(row_t[:, 0:ECP], bank[0][:, 0:ECP], ACT.Copy)
            act.activation(dst_t[:, 0:ECP], bank[1][:, 0:ECP], ACT.Copy)
            act.activation(norm_t[:, 0:ECP], bank[2][:, 0:ECP], ACT.Copy).then_inc(table_rdy, 1)

            y_stored(act)

            def high_part(h):
                _, stage, high, _ = half(h)
                act.wait_ge(ld_w[h % STAGES], 16 * (h // STAGES + 1))
                act.activation(high, stage, ACT.Copy).then_inc(w_h, 1)

            def gelu(g, e, tiles):
                cols = tiles * SLOT + tiles * SLOT % 2
                if not (isinstance(g, int) and g == 0 and e < 2):
                    if e:
                        act.wait_ge(y2_mm, outputs(g, e - 1, 0, tiles) + GT)
                    else:
                        act.wait_ge(y2_mm, outputs(g, 0, 0, tiles) + (GT - 1 if isinstance(g, int) and g == 1 else 0))
                for hc in range(HC):
                    bank_of, _ = hidden_bank(e, hc, tiles)
                    act.wait_ge(h_mm, g * (X * HC) + e * HC + hc + 1)
                    act.activation(hidden[:, e % 2, hc, 0:cols], bank_of[:, 0:cols], ACT.Gelu,
                                   bias=b1_s[:, e, hc:hc + 1])
                    act.activation(hh[:, e % 2, hc, 0:cols], bank_of[:, 0:cols], ACT.Gelu,
                                   bias=b1_s[:, e, hc:hc + 1]).then_inc(h_act, 1)

            def tanh_of_gap(g, tiles):
                act.wait_ge(dlt_rdy, g + 1)
                act.activation(tnh[0:TN, 0:tiles], dlt[0:TN, 0:tiles], ACT.Tanh, scale=0.5).then_inc(tnh_rdy, 1)

            def experts(g, par, tiles, ahead):
                for e in range(X):
                    if e + 1 < X:
                        gelu(g, e + 1, tiles)
                    elif ahead:
                        tanh_of_gap(g + 1, ahead)
                        gelu(g + 1, 0, ahead)

            act.wait_ge(ld_small, 16 * n_small)
            for h in range(HALVES):
                high_part(h)
            act.wait_ge(early_done, 1)
            act.wait_ge(w_l, HALVES)
            tanh_of_gap(0, 1)
            gelu(0, 0, 1)
            experts(0, 0, 1, GT)
            with act.Fori(0, (NG - 2) // 2) as i:
                for j in range(2):
                    experts(i * 2 + j + 1, (j + 1) % 2, GT, GT)
            experts(NG - 1, 1, GT, GT)
            experts(NG, 0, GT, 0)

        @block.vector
        def _(dve):
            seq = dve.alloc_register("dve_steps")
            dve.reg_mov(seq, 0)

            def chain(*steps):
                for step in steps:
                    step().then_inc(dve_seq, 1)
                    dve.reg_add(seq, seq, 1)
                    dve.wait_ge(dve_seq, dve.snap(seq, min_val=0, max_val=1 << 20))
                    dve.sem_inc(dve_go, 1)

            def rsqrt_steps(rows, n):
                v, r, t = ve[0:rows, 0:n], rs[0:rows, 0:n], rt[0:rows, 0:n]
                steps = [
                    lambda: dve.tensor_scalar(r.bitcast(I32), v.bitcast(I32), 1, None, ALU.logical_shift_right),
                    lambda: dve.tensor_scalar(r.bitcast(I32), r.bitcast(I32), -1.0, float(0x5F3759DF),
                                              ALU.mult, ALU.add),
                ]
                for _ in range(3):
                    steps += [
                        lambda: dve.tensor_tensor(t, r, r, ALU.mult),
                        lambda: dve.scalar_tensor_tensor(out=t, in0=t, scalar=-0.5, in1=v, op0=ALU.mult, op1=ALU.mult),
                        lambda: dve.scalar_tensor_tensor(out=r, in0=t, scalar=1.5, in1=r, op0=ALU.add, op1=ALU.mult),
                    ]
                return steps

            def each(tiles, f):
                def step():
                    for k in range(tiles):
                        last = f(k)
                    return last
                return step

            def first_statistics(rows, tiles, source, stat):
                chain(each(tiles, lambda k: dve.bn_stats(stat[0:rows, k, :], source(k))))

            def rest_of_statistics(rows, tiles, stat, a=1.0, b=EPS):
                chain(
                    each(tiles, lambda k: dve.bn_aggr(mv[0:rows, k, :], stat[0:rows, k, :])),
                    lambda: dve.tensor_scalar(ve[0:rows, 0:tiles], mv[0:rows, 0:tiles, 1], a, b, ALU.mult,
                                              ALU.add),
                    *rsqrt_steps(rows, tiles),
                )

            def centre(rows, k, source, target):
                return dve.tensor_scalar(target, source, mv[0:rows, k, 0:1], rs[0:rows, k:k + 1],
                                         ALU.subtract, ALU.mult)

            dve.sem_inc(y2_add, GT + PAD * X)
            for counts_tiles in (x1_rdy, iota_rdy, xt_rdy, b_add):
                dve.sem_inc(counts_tiles, PAD)
            dve.sem_inc(t_read, 1)
            dve.memset(wraw[:, :, :, :], 0.0).then_inc(fill, 1)
            dve.memset(e_src[:, EB - 1, :], 0)
            dve.memset(e_rel[:, EB - 1, :], 0)
            dve.memset(e_dst[:, EB - 1, :], N - 1)
            dve.memset(xall[:, FULL, :], 0.0)
            dve.memset(e_norm[:, EB - 1, :], 0.0).then_inc(fill, 1)
            dve.memset(ones[:, :], 1.0)
            dve.memset(zero_r[:, :].bitcast(F32), 0.0)
            dve.memset(span_lo[:, :], 0)
            dve.memset(span_n[:, :], NEVER)

            def make_spans():
                dve.wait_ge(pe_edge, 2 * EB)
                dve.wait_ge(ld_small, 16 * n_small)
                chain(
                    lambda: dve.tensor_scalar(ends[:, 1:2], ends[:, 0:1], float(TN), None, ALU.add),
                    lambda: dve.tensor_scalar(hit[:, :], bank[7][0:NT, 0:EC], ends[:, 0:1], None, ALU.is_ge),
                    lambda: dve.scalar_tensor_tensor(out=hit[:, :], in0=bank[6][0:NT, 0:EC], scalar=ends[:, 1:2],
                                                     in1=hit[:, :], op0=ALU.is_lt, op1=ALU.mult),
                    lambda: dve.scalar_tensor_tensor(out=hit2[:, :], in0=iota_t[:, :], scalar=1.0, in1=hit[:, :],
                                                     op0=ALU.add, op1=ALU.mult),
                    lambda: dve.tensor_reduce(lohi[:, 1:2], hit2[:, :], AX.X, ALU.max),
                    lambda: dve.scalar_tensor_tensor(out=hit2[:, :], in0=hit[:, :], scalar=-FAR, in1=iota_t[:, :],
                                                     op0=ALU.mult, op1=ALU.add),
                    lambda: dve.tensor_reduce(lohi[:, 0:1], hit2[:, :], AX.X, ALU.min),
                    lambda: dve.tensor_scalar(lohi[:, 2:3], lohi[:, 0:1], FAR, float(EC - 1), ALU.add, ALU.min),
                    lambda: dve.scalar_tensor_tensor(out=lohi[:, 3:4], in0=lohi[:, 1:2], scalar=QC - 1.0,
                                                     in1=lohi[:, 2:3], op0=ALU.add, op1=ALU.subtract),
                    lambda: dve.tensor_scalar(lohi_i[:, 0:1], lohi[:, 3:4], least_s[:, 0:1], None, ALU.max),
                    lambda: dve.tensor_scalar(lohi_i[:, 1:2], lohi_i[:, 0:1], 2, None, ALU.arith_shift_right),
                )
                dve.tensor_copy(lohi[:, 3:4], lohi_i[:, 1:2]).then_inc(span_col, 1)
                dve.wait_ge(pe_edge, 4 + 2 * EB)
                dve.tensor_copy(span_lo[:, 0:NT], bank[6][0:1, 0:NT])
                chain(
                    lambda: dve.tensor_reduce(hit[0:1, 0:1], bank[6][0:1, 32:32 + NT], AX.X, ALU.add),
                    lambda: dve.tensor_scalar(turns_s[:, 0:1], hit[0:1, 0:1], RING - 1.0, None, ALU.add),
                    lambda: dve.tensor_scalar(turns_s[:, 1:2], turns_s[:, 0:1], RING.bit_length() - 1, None,
                                              ALU.arith_shift_right),
                )
                dve.tensor_copy(span_n[:, 0:NT], bank[6][0:1, 32:32 + NT]).then_inc(span_rdy, 1)
                dve.wait_ge(span_rdy, 1)
                dve.wait_ge(table_rdy, 1)

            def loaded_x(k):
                if k % (FULL // 4) == 0:
                    dve.wait_ge(ld_x[k // (FULL // 4)], 16)
                return xall[:, k, :]

            first_statistics(P, FULL + 1, loaded_x, stat_x)
            rest_of_statistics(P, FULL + 1, stat_x)
            def normalise_x(t, par):
                if not (isinstance(t, int) and t < 2):
                    dve.wait_ge(xp_t, t - 1)
                at = bass.ds(t, 1)
                dve.tensor_scalar(xnorm[:, par, :], xall[:, at, :].rearrange("p a d -> p (a d)"),
                                  mv[:, at, 0], rs[:, at], ALU.subtract, ALU.mult).then_inc(xhat_rdy, 1)

            def low_part(t, par):
                dve.wait_ge(xp_h, t + 1)
                dve.tensor_tensor(xpl[:, par, :, :].rearrange("p c n -> p (c n)"), bank_tp[par][:, 0:D],
                                  xph[:, par, :, :].rearrange("p c n -> p (c n)"), ALU.subtract).then_inc(xp_l, 1)

            def copy_y(t, j, u):
                dve.wait_ge(y_mm, t * 4 + u + 1)
                dve.tensor_copy(ybuf[:, j, 4:8, u // 2, :],
                                bank_y[u][:, :].rearrange("p (r g) -> p r g", g=P)).then_inc(y_ev_v, 1)

            def tile_y(i, j):
                t = i * YB + j
                if not (isinstance(t, int) and t + 2 > FULL):
                    normalise_x(t + 2, j % 2)
                if not (isinstance(t, int) and t + 1 > FULL):
                    low_part(t + 1, (j + 1) % 2)
                if not (isinstance(i, int) and i == 0):
                    dve.wait_ge(y_st[j], i * 16)
                copy_y(t, j, 1)
                copy_y(t, j, 3)

            normalise_x(0, 0)
            normalise_x(1, 1)
            low_part(0, 0)

            dve.wait_ge(ld_edge, 16 * 12)
            dve.tensor_copy(rowf[:, :, :], e_src[:, :, :])
            dve.tensor_copy(dstf[:, :, :], e_dst[:, :, :]).then_inc(edge_f, 1)
            dve.wait_ge(edge_f, 1)
            dve.tensor_reduce(mnmx[:, 0, :], dstf[:, :, :], AX.X, ALU.min)
            dve.tensor_reduce(mnmx[:, 1, :], dstf[:, :, :], AX.X, ALU.max).then_inc(edge_f, 1)
            dve.scalar_tensor_tensor(out=rowf[:, :, :], in0=rowf[:, :, :], scalar=float(R), in1=e_rel[:, :, :],
                                     op0=ALU.mult, op1=ALU.add).then_inc(edge_f, 1)
            dve.wait_ge(edge_f, 3)
            dve.wait_ge(pool_const, 5)
            for i in range(2 * EB):
                dve.tensor_scalar(diag[:, i, :], ident[:, :], mnmx[:, i // EB, i % EB:i % EB + 1], None,
                                  ALU.mult).then_inc(diag_rdy, 1)

            for j in range(YB):
                tile_y(0, j)
            with dve.Fori(1, FULL // YB - 1) as i:
                for j in range(YB):
                    tile_y(i, j)
            for t in range(FULL - YB, FULL + 1):
                tile_y(t // YB, t % YB)
            make_spans()

            y_stored(dve)
            for t in (xth, xtl):
                last = dve.memset(t[:, :, :, SLOT:COLS:2 * SLOT].bitcast(F32), 0.0)
            last.then_inc(early_done, 1)

            def low_part_of_half(h):
                _, stage, high, low = half(h)
                dve.wait_ge(w_h, h + 1)
                dve.tensor_tensor(low, stage, high, ALU.subtract).then_inc(w_l, 1)

            batch = dve.alloc_register("dve_batch")
            ecol = dve.alloc_register("dve_col")
            left = dve.alloc_register("dve_left")
            dve.reg_mov(batch, 0)

            def match_batch(m_set, again):
                b = dve.snap(batch, min_val=0, max_val=NEVER * NT)
                c = dve.snap(ecol, min_val=0, max_val=ECP - QC)
                if not again:
                    dve.wait_ge(m_used, b * QC + 1)
                for j in range(QC):
                    if again:
                        dve.wait_ge(m_used, b * QC + (j + 2))
                    dve.tensor_scalar(m_s[:, m_set * QC + j, :], iota_s[:, :], dst_t[:, bass.ds(c + j, 1)],
                                      norm_t[:, bass.ds(c + j, 1)], ALU.is_equal, ALU.mult).then_inc(m_rdy, 1)
                dve.reg_add(batch, batch, 1)
                dve.reg_add(ecol, ecol, QC)

            def match_first(g, k, part, parts, m_set):
                if part == 0:
                    dve.reg_load(ecol, span_lo[0:1, bass.ds(place_of(g, k), 1)])
                    if not (isinstance(g, int) and g == 0):
                        dve.wait_ge(m_rdy, dve.snap(batch, min_val=1, max_val=NEVER * NT) * QC)
                    dve.tensor_scalar(iota_s[:, :], iota[:, :], starts[:, bass.ds(place_of(g, k), 1)], None,
                                      ALU.add).then_inc(iota_rdy, 1)
                    dve.wait_ge(iota_rdy, count(g, k) + 1)
                    dve.sem_inc(dve_go, 1)
                match_batch(m_set, False)
                dve.reg_mov(left, part_of(dve, g, k, part, parts))
                with dve.If_ne(left, 1):
                    match_batch(2, False)

            def match_rest():
                with dve.If_ne(left, 1):
                    with dve.If_ne(left, 2):
                        with dve.Fori(2, dve.snap(left, min_val=3, max_val=NEVER)):
                            match_batch(2, True)
                        dve.sem_inc(dve_go, 1)
                    dve.sem_inc(dve_go, 1)

            def take_x1(g, par, k):
                dve.wait_ge(ld_xin[k], g * 16 + 16)
                if not (isinstance(g, int) and g < 2):
                    dve.wait_ge(st_out[k], g * 16)
                dve.wait_ge(m_used, dve.snap(batch, min_val=1, max_val=NEVER * NT) * QC + (QC + 1))
                dve.tensor_tensor(x1[0:TN, par, k, :], bank_acc[0:TN, 0:D], xz[0:TN, k, :],
                                  ALU.add).then_inc(x1_rdy, 1)

            def both_statistics(g, par, tiles):
                dve.wait_ge(x1_rdy, g * GT + GT)
                first_statistics(TN, tiles, lambda k: x1[0:TN, par, k, :], stat)
                rest_of_statistics(TN, tiles, stat, 1.0 + EPS, EPS * EPS)

            def normalise(g, par, tiles):
                each(tiles, lambda k: centre(TN, k, x1[0:TN, par, k, :], xz[0:TN, k, :]))().then_inc(z_rdy, 1)

            def activations(g, par, first, tiles):
                last_k = min(first + 2, tiles)
                dve.wait_ge(t_made, use_of(g, first // 2) + 1)
                for k in range(first, last_k):
                    for c in range(DC):
                        at = (k - first) * D + c * P
                        last = dve.tensor_scalar(xtf[:, c, k * SLOT:k * SLOT + TN], bank_t[:, at:at + TN],
                                                 gam[:, c:c + 1], bet[:, c:c + 1], ALU.mult, ALU.add)
                last.then_inc(t_read, 1)
                dve.wait_ge(t_read, use_of(g, first // 2) + 1)
                for k in range(first, last_k):
                    f = slice(k * SLOT, k * SLOT + TN)
                    last = dve.tensor_copy(xth[:, par, :, f], xtf[:, :, f])
                chain(lambda: last)
                for k in range(first, last_k):
                    f = slice(k * SLOT, k * SLOT + TN)
                    dve.tensor_tensor(xtl[:, par, :, f], xtf[:, :, f], xth[:, par, :, f],
                                      ALU.subtract).then_inc(xt_rdy, 1)

            def rank(g, tiles):
                use = (tiles + 1) // 2
                dve.wait_ge(t_made, use_of(g, use) + 1)
                for k in range(tiles):
                    last = dve.tensor_tensor(logit[0:TN, k, :], bank_t[0:TN, k * X:(k + 1) * X], br_s[0:TN, :], ALU.add)
                last.then_inc(t_read, 1)
                dve.wait_ge(t_read, use_of(g, use) + 1)
                dve.sem_inc(dve_go, 1)
                chain(
                    each(tiles, lambda k: dve.max(mx8[0:TN, k, :], logit[0:TN, k, :])),
                    each(tiles, lambda k: dve.max_index(ix8[0:TN, k, :], mx8[0:TN, k, :], logit[0:TN, k, :])),
                )
                dve.tensor_tensor(dlt[0:TN, 0:tiles], mx8[0:TN, 0:tiles, 0], mx8[0:TN, 0:tiles, 1],
                                  ALU.subtract).then_inc(dlt_rdy, 1)
                dve.tensor_copy(ixf[0:TN, 0:tiles, :], ix8[0:TN, 0:tiles, :])

            def weigh(g, tiles):
                dve.wait_ge(tnh_rdy, g + 1)
                if not (isinstance(g, int) and g == 0):
                    dve.wait_ge(y2_add, g * (GT * X) + GT)
                chain(
                    each(2, lambda i: dve.tensor_scalar(w12[0:TN, i, 0:tiles], tnh[0:TN, 0:tiles],
                                                        (0.5, -0.5)[i], 0.5, ALU.mult, ALU.add)),
                    lambda: (each(tiles, lambda k: dve.tensor_scalar(
                        wfull[0:TN, k, :], iota8[0:TN, :], ixf[0:TN, k, 0:1], w12[0:TN, 0, k:k + 1],
                        ALU.is_equal, ALU.mult))(),
                        each(tiles, lambda k: dve.tensor_scalar(
                            logit[0:TN, k, :], iota8[0:TN, :], ixf[0:TN, k, 1:2], w12[0:TN, 1, k:k + 1],
                            ALU.is_equal, ALU.mult))())[1],
                )
                dve.tensor_tensor(wfull[0:TN, 0:tiles, :], wfull[0:TN, 0:tiles, :], logit[0:TN, 0:tiles, :],
                                  ALU.add).then_inc(wf_rdy, 1)

            def take_weights(g, tiles):
                use = (tiles + 1) // 2 + 1
                dve.wait_ge(t_made, use_of(g, use) + 1)
                for k in range(tiles):
                    last = dve.tensor_copy(wft[:, k * SLOT:k * SLOT + TN], bank_t[0:X, k * SLOT:k * SLOT + TN])
                last.then_inc(wft_rdy, 1)
                dve.wait_ge(wft_rdy, g + 1)
                dve.sem_inc(t_read, 1)

            def add_bias2(g, par, tiles):
                for k in range(tiles):
                    dve.wait_ge(b_mm, count(g, k) + 1)
                    dve.wait_ge(y2_add, outputs(g, 0, k, tiles) + (GT + 1))
                    dve.tensor_tensor(x1[0:TN, par, k, :], bank_o[k][0:TN, 0:D], x1[0:TN, par, k, :],
                                      ALU.add).then_inc(b_add, 1)

            def low_parts(g, e, tiles):
                cols = tiles * SLOT + tiles * SLOT % 2
                for hc in range(HC):
                    dve.wait_ge(h_act, g * (X * HC) + e * HC + hc + 1)
                    dve.tensor_tensor(hl[:, e % 2, hc, 0:cols], hidden[:, e % 2, hc, 0:cols],
                                      hh[:, e % 2, hc, 0:cols], ALU.subtract).then_inc(h_split, 1)

            def add(g, par, e, tiles):
                for k in range(tiles):
                    dve.wait_ge(y2_mm, outputs(g, e, k, tiles) + (GT + 1))
                    if e == 1:
                        dve.wait_ge(b_add, count(g, k) + 1)
                    elif e:
                        dve.wait_ge(y2_add, outputs(g, e - 1, k, tiles) + (GT + 1))
                    dve.scalar_tensor_tensor(out=x1[0:TN, par, k, :], in0=bank_o[k][0:TN, 0:D],
                                             scalar=wfull[0:TN, k, e:e + 1], in1=x1[0:TN, par, k, :],
                                             op0=ALU.mult, op1=ALU.add).then_inc(y2_add, 1)

            places = list(PARTS)

            def begin_part(g, i, tiles):
                if i < len(places) and PARTS[places[i]][0] < tiles:
                    k, part = PARTS[places[i]]
                    match_first(g, k, part, PIECES[k], i % 2)

            def experts(g, par, tiles, ahead, ahead2):
                def match(e, place):
                    k, part = PARTS.get((e, place), (GT, 0))
                    if k < ahead:
                        i = places.index((e, place))
                        match_rest()
                        if part == PIECES[k] - 1:
                            take_x1(g + 1, 1 - par, k)
                        begin_part(g + 1, i + 1, ahead)

                for e in range(X):
                    match(e, "up")
                    if e == 1:
                        add_bias2(g, par, tiles)
                    if e == X - 3 and ahead:
                        both_statistics(g + 1, 1 - par, ahead)
                        normalise(g + 1, 1 - par, ahead)
                    if e == X - 2 and ahead:
                        activations(g + 1, 1 - par, 0, ahead)
                    if e == X - 1 and ahead:
                        rank(g + 1, ahead)
                    if e + 1 < X:
                        low_parts(g, e + 1, tiles)
                    elif ahead:
                        low_parts(g + 1, 0, ahead)
                    match(e, "down")
                    if e == 0:
                        take_weights(g, tiles)
                    if e == X - 2 and ahead > 2:
                        activations(g + 1, 1 - par, 2, ahead)
                    if e == X - 1 and ahead2:
                        begin_part(g + 2, 0, ahead2)
                    add(g, par, e, tiles)
                if ahead:
                    weigh(g + 1, ahead)

            match_first(0, 0, 0, 1, 1)
            for h in range(STAGES + 2):
                low_part_of_half(h)
            match_rest()
            for h in range(STAGES + 2, 2 * STAGES + 2):
                low_part_of_half(h)
            take_x1(0, 0, 0)
            both_statistics(0, 0, 1)
            normalise(0, 0, 1)
            for h in range(2 * STAGES + 2, HALVES):
                low_part_of_half(h)
            activations(0, 0, 0, 1)
            rank(0, 1)
            low_parts(0, 0, 1)
            begin_part(1, 0, GT)
            weigh(0, 1)
            experts(0, 0, 1, GT, GT)
            with dve.Fori(0, (NG - 2) // 2) as i:
                for j in range(2):
                    experts(i * 2 + j + 1, (j + 1) % 2, GT, GT, GT)
            experts(NG - 1, 1, GT, GT, 0)
            experts(NG, 0, GT, 0, 0)


def kernel(x, src, dst, edge_type_8, edge_weight, L0_gnn_weight, L0_ffn_gamma, L0_ffn_beta, L0_ffn_Wr, L0_ffn_br,
           L0_ffn_W1, L0_ffn_b1, L0_ffn_W2, L0_ffn_b2):
    from concourse import bacc
    from concourse.bass_utils import run_bass_kernel_spmd

    first_nodes = TN * np.array(ORDER)
    ins = {
        "x": x, "src": src, "dst": dst, "rel": edge_type_8, "norm": edge_weight,
        "gnn_w": np.asarray(L0_gnn_weight).reshape(R, NB * SB * SB), "gamma": L0_ffn_gamma, "beta": L0_ffn_beta,
        "wr": L0_ffn_Wr, "br": L0_ffn_br, "w1": L0_ffn_W1, "b1": L0_ffn_b1, "w2": L0_ffn_W2, "b2": L0_ffn_b2,
        "starts_f": first_nodes.astype(np.float32), "starts_i": first_nodes.astype(np.int32).reshape(1, NT),
        "least": QC * np.array([SHORTEST] + [LEAST[i % GT] for i in range(NT - 1)], np.float32),
    }
    ins = {name: np.ascontiguousarray(a) for name, a in ins.items()}
    nc = bacc.Bacc("TRN2", target_bir_lowering=False, num_devices=1)
    aps = {name: nc.dram_tensor(f"in_{name}", a.shape, mybir.dt.from_np(a.dtype), kind="ExternalInput").ap()
           for name, a in ins.items()}
    out = nc.dram_tensor("out_x", (N, D), F32, kind="ExternalOutput").ap()
    build_program(nc, out=out, **aps)
    r = run_bass_kernel_spmd(nc, [{f"in_{name}": a for name, a in ins.items()}], core_ids=[0])
    return r.results[0]["out_x"]
```
